# Optimizing a Trainium2 kernel written in Bass

```python
import numpy as np
import jax
import jax.numpy as jnp

def _softmax(x, axis=-1):
    return jax.nn.softmax(x, axis=axis)

def _gelu(x):
    return jax.nn.gelu(x, approximate=True)

def _silu(x):
    return jax.nn.silu(x)

def _sigmoid(x):
    return jax.nn.sigmoid(x)

def _layernorm(x, axis=-1, eps=1e-05):
    m = jnp.mean(x, axis=axis, keepdims=True)
    v = jnp.var(x, axis=axis, keepdims=True)
    return (x - m) / jnp.sqrt(v + eps)

def _scatter_add(tgt, idx, src, axis=0):
    return tgt.at[idx].add(src)

def _segment_sum(src, seg, n):
    return jax.ops.segment_sum(src, seg, n)
kernel_name = 'mk_adaln_ffn_d1_seqx_r8_f11693'

def setup_inputs(seed: int=0):
    np.random.seed(seed)
    _w = jnp.asarray

    def _rec_inputs():
        import jax
        import jax.numpy as jnp
        _rk = jax.random.key(seed)
        x = 7.22e-05 + 1 * jax.random.normal(jax.random.fold_in(_rk, 1), (8, 128, 512), jnp.float32)
        _lenS = 128 - jax.random.randint(jax.random.fold_in(_rk, 7), (8,), 0, max(1, 128 // 4) + 1, jnp.int32)
        _lenS2 = 128 - jax.random.randint(jax.random.fold_in(_rk, 8), (8,), 0, max(1, 128 // 4) + 1, jnp.int32)
        itok_B_2_6 = jax.random.randint(jax.random.fold_in(_rk, 11), (8,), 2, 7, jnp.int32)
        return (x, itok_B_2_6)
    x, itok_B_2_6 = _rec_inputs()

    def _L0_cond_setup():
        import jax, jax.numpy as jnp
        import numpy as np
        B, N, H, F = (4, 64, 512, 1376)
        L, R, RANK = (1, 16, 16)
        SCALE = 0.5
        key = jax.random.key(seed)
        ks = jax.random.split(key, 12)
        nrm = lambda k, shape, fan: jax.random.normal(k, shape, jnp.float32) * fan ** (-0.5)
        inp = {'x': jax.random.normal(ks[0], (B, N, H), jnp.float32), 'W_gate': nrm(ks[1], (F, H), H), 'W_up': nrm(ks[2], (F, H), H), 'W_down': nrm(ks[3], (H, F), F), 'A_gate': nrm(ks[4], (L, R, RANK, H), H), 'B_gate': nrm(ks[5], (L, R, F, RANK), RANK), 'A_up': nrm(ks[6], (L, R, RANK, H), H), 'B_up': nrm(ks[7], (L, R, F, RANK), RANK), 'A_down': nrm(ks[8], (L, R, RANK, F), F), 'B_down': nrm(ks[9], (L, R, H, RANK), RANK), 'lora_indices': jax.random.randint(ks[10], (B,), 0, R), 'layer_idx': 0}
        return inp
    _L0_cond_all = _L0_cond_setup()
    _L0_cond_in = {k: v for k, v in _L0_cond_all.items() if k in ('W_gate', 'W_up', 'W_down', 'A_gate', 'B_gate', 'A_up', 'B_up', 'A_down', 'B_down')}
    del _L0_cond_all

    def _L0_ffn_setup():
        import jax, jax.numpy as jnp
        import numpy as np
        GROUP_SIZE = 128

        def dequantize_int4(weight_q, scale, zero_point, group_size):
            out_f, in_f = weight_q.shape
            n_groups = in_f // group_size
            w = weight_q.astype(jnp.float32).reshape(out_f, n_groups, group_size)
            w = (w - zero_point[:, :, None]) * scale[:, :, None]
            return w.reshape(out_f, in_f)
        key = jax.random.key(seed)
        k1, k2, k3, k4, k5 = jax.random.split(key, 5)
        B, S, D_IN, D_OUT = (2, 256, 512, 512)
        n_groups = D_IN // GROUP_SIZE
        x = jax.random.normal(k1, (B, S, D_IN), dtype=jnp.float32)
        weight_q = jax.random.randint(k2, (D_OUT, D_IN), 0, 16, dtype=jnp.int32)
        scale = jax.random.uniform(k3, (D_OUT, n_groups), dtype=jnp.float32, minval=0.001, maxval=0.02)
        zero_point = jax.random.uniform(k4, (D_OUT, n_groups), dtype=jnp.float32, minval=0.0, maxval=15.0)
        bias = jax.random.normal(k5, (D_OUT,), dtype=jnp.float32)
        return {'x': x, 'weight_q': weight_q, 'scale': scale, 'zero_point': zero_point, 'bias': bias}
    _L0_ffn_all = _L0_ffn_setup()
    _L0_ffn_in = {k: v for k, v in _L0_ffn_all.items() if k in ('weight_q', 'scale', 'zero_point', 'bias')}
    del _L0_ffn_all
    return {'x': x, 'itok_B_2_6': itok_B_2_6, 'L0_cond_W_gate': _L0_cond_in['W_gate'], 'L0_cond_W_up': _L0_cond_in['W_up'], 'L0_cond_W_down': _L0_cond_in['W_down'], 'L0_cond_A_gate': _L0_cond_in['A_gate'], 'L0_cond_B_gate': _L0_cond_in['B_gate'], 'L0_cond_A_up': _L0_cond_in['A_up'], 'L0_cond_B_up': _L0_cond_in['B_up'], 'L0_cond_A_down': _L0_cond_in['A_down'], 'L0_cond_B_down': _L0_cond_in['B_down'], 'L0_ffn_weight_q': _L0_ffn_in['weight_q'], 'L0_ffn_scale': _L0_ffn_in['scale'], 'L0_ffn_zero_point': _L0_ffn_in['zero_point'], 'L0_ffn_bias': _L0_ffn_in['bias']}

def reference(x, itok_B_2_6, L0_cond_W_gate, L0_cond_W_up, L0_cond_W_down, L0_cond_A_gate, L0_cond_B_gate, L0_cond_A_up, L0_cond_B_up, L0_cond_A_down, L0_cond_B_down, L0_ffn_weight_q, L0_ffn_scale, L0_ffn_zero_point, L0_ffn_bias):
    import jax
    import jax.numpy as jnp

    def _L0_cond_ref(x, W_gate, W_up, W_down, A_gate, B_gate, A_up, B_up, A_down, B_down, lora_indices, layer_idx):
        import jax, jax.numpy as jnp
        import numpy as np
        B, N, H, F = (4, 64, 512, 1376)
        L, R, RANK = (1, 16, 16)
        SCALE = 0.5

        def lora_add(base, inp, A, B):
            Ab = A[layer_idx][lora_indices]
            Bb = B[layer_idx][lora_indices]
            t = jnp.einsum('bri,bni->bnr', Ab, inp)
            return base + jnp.einsum('bor,bnr->bno', Bb, t) * SCALE
        gate = lora_add(jnp.einsum('bnh,fh->bnf', x, W_gate), x, A_gate, B_gate)
        up = lora_add(jnp.einsum('bnh,fh->bnf', x, W_up), x, A_up, B_up)
        act = jax.nn.silu(gate) * up
        down = lora_add(jnp.einsum('bnf,hf->bnh', act, W_down), act, A_down, B_down)
        return down

    def _L0_ffn_ref(x, weight_q, scale, zero_point, bias):
        import jax, jax.numpy as jnp
        import numpy as np
        GROUP_SIZE = 128

        def dequantize_int4(weight_q, scale, zero_point, group_size):
            out_f, in_f = weight_q.shape
            n_groups = in_f // group_size
            w = weight_q.astype(jnp.float32).reshape(out_f, n_groups, group_size)
            w = (w - zero_point[:, :, None]) * scale[:, :, None]
            return w.reshape(out_f, in_f)
        w = dequantize_int4(weight_q, scale, zero_point, GROUP_SIZE).astype(x.dtype)
        return jnp.einsum('bsi,oi->bso', x, w) + bias
    x = x + _L0_ffn_ref(_L0_cond_ref(x, L0_cond_W_gate, L0_cond_W_up, L0_cond_W_down, L0_cond_A_gate, L0_cond_B_gate, L0_cond_A_up, L0_cond_B_up, L0_cond_A_down, L0_cond_B_down, itok_B_2_6, 0), L0_ffn_weight_q, L0_ffn_scale, L0_ffn_zero_point, L0_ffn_bias)
    return x

_drawn_inputs = setup_inputs


def setup_inputs(seed=0):
    import zlib

    import numpy as np

    out = dict(_drawn_inputs(seed))
    spreads = {}
    factors = {}
    for name, (base, spread) in spreads.items():
        noise = np.random.default_rng([zlib.crc32(name.encode()), seed]).standard_normal(out[name].shape)
        drawn = base * np.exp(spread * noise) if base else spread * noise
        out[name] = jnp.asarray(drawn.astype(out[name].dtype))
    for name, factor in factors.items():
        out[name] = (out[name] * factor).astype(out[name].dtype)
    return out
```

```python
from contextlib import ExitStack

import concourse.bass as bass
from concourse import mybir

F32 = mybir.dt.float32
F32R = mybir.dt.float32r
I32 = mybir.dt.int32
ALU = mybir.AluOpType
ACT = mybir.ActivationFunctionType

P = 128
Q = 32
NB, T, H, F, R = 8, 128, 512, 1376, 16
NT = NB * T
HALF = NT // 2
KT = H // P
FB = F // Q
FT = -(-FB // 4)
FQ = FT * Q
F3 = 3 * FQ
LAST = F - F3
NL = LAST // Q
KL = 3 * Q
PAIRS = NB // 2
PT = 2 * T
LORA_SCALE = 0.5
PROLOGUE_TILES = 2


def adaln_ffn(nc, x, idx, w_gate, w_up, w_down, a_gate, b_gate, a_up, b_up, a_down, b_down,
              wq, scale, zero_point, bias, out):
    gu_w = (w_gate, w_up)
    gu_a = (a_gate, a_up)
    gu_b = (b_gate, b_up)
    x_flat = x.rearrange("b t h -> (b t) h")
    out_flat = out.rearrange("b t h -> (b t) h")
    idx_row = idx.rearrange("(a b) -> a b", a=1)

    with ExitStack() as ctx:
        size = 212736
        arena = ctx.enter_context(nc.sbuf_tensor("arena", [P, size // 4], F32))
        base = nc.sbuf_base - size
        base = (base + 31) // 32 * 32
        places = {}
        top = [0]

        def room(name, nbytes):
            places[name] = base + top[0]
            top[0] += nbytes
            assert top[0] <= size, (name, top[0])

        def at(name, place, shape, dt=F32, plus=0):
            return nc.alloc_sbuf_tensor_at(name, shape, dt, offset=places[place] + plus)

        room("tokens", 2 * KT * NT * 4)
        room("act", 2 * FT * NT * 4)
        room("wring", 2 * 2 * 2 * KT * P * 4)
        room("wx", 2 * 2 * KT * P * 4)
        room("wy", 2 * KT * P * 4)
        room("temps", 4 * HALF * 4)
        room("by", 2 * FQ * 4 * 4)
        room("bhl", 2 * 2 * P * 4)
        room("sring", 2 * PAIRS * 2 * P * 4)
        room("ady", PAIRS * FQ * 4)
        room("adring", 2 * 2 * P * 4)
        room("tstack", 2 * NT * 4)
        room("wd0", 2 * (FT - 1) * P * 4 + PAIRS * 2 * P * 4)
        room("mask", PT * 4)
        room("sz", 2 * 4 * KT * 4)

        xt_hi = at("xt_hi", "tokens", [P, KT, NT], F32R)
        xt_lo = at("xt_lo", "tokens", [P, KT, NT], F32R, KT * NT * 4)
        dt_hi = at("dt_hi", "tokens", [P, KT, NT], F32R)
        dt_lo = at("dt_lo", "tokens", [P, KT, NT], F32R, KT * NT * 4)
        act_hi = at("act_hi", "act", [P, FT, NT], F32R)
        act_lo = at("act_lo", "act", [P, FT, NT], F32R, FT * NT * 4)
        early = 2 * NT * 4
        x_in = at("x_in", "act", [P, NT // Q, P], F32, early)
        x_tr = at("x_tr", "act", [P, KT, NT], F32, early + 16384)
        a_in = at("a_in", "act", [P, 2, H], F32, early + 32768)
        low = FT * NT * 4 + early
        b_in = at("b_in", "act", [P, 2, 2, FB * R], F32, low)
        a_hi = at("a_hi", "act", [P, KT, PAIRS, 2, Q], F32R, low + 11264)
        a_lo = at("a_lo", "act", [P, KT, PAIRS, 2, Q], F32R, low + 11264 + 4096)
        ad_in = at("ad_in", "act", [P, PAIRS, FQ], F32, low + 11264 + 8192)
        ident = at("ident", "act", [P, P], F32, low + 11264 + 8192 + 5632)
        a_perm = at("a_perm", "act", [P, 2, KT, P], F32, low + 11264 + 8192 + 5632 + 512)
        w_in = at("w_in", "wx", [P, 2, 2, 4, P])
        w_tr = at("w_tr", "wy", [P, 2, KT, P])
        w_hi = at("w_hi", "wring", [P, 2, 2, KT, P], F32R)
        w_lo = at("w_lo", "wring", [P, 2, 2, KT, P], F32R, 2 * 2 * KT * P * 4)
        silu = at("silu", "temps", [P, 2, HALF])
        actf = at("actf", "temps", [P, 2, HALF], F32, 2 * HALF * 4)
        b_tr = at("b_tr", "by", [P, 2, 4 * FQ])
        b_hi = at("b_hi", "bhl", [P, 2, P], F32R)
        b_lo = at("b_lo", "bhl", [P, 2, P], F32R, 2 * P * 4)
        b_stack = at("b_stack", "sring", [P, 2, PAIRS, 2, P], F32R)
        ad_tr = at("ad_tr", "ady", [P, PAIRS, FT, Q])
        ad_parts = at("ad_parts", "adring", [P, 2, 2, 2, 2, Q], F32R)
        t_stack = at("t_stack", "tstack", [P, 2, NT], F32R)
        bd_tr = at("bd_tr", "tstack", [P, PAIRS, KT, P])
        bd_in = at("bd_in", "wd0", [P, PAIRS, 2, 4, KT * R])
        t_val = at("t_val", "wd0", [P, 2, PT], F32, 8192)
        t_hi = at("t_hi", "wd0", [P, 2, PT], F32R, 8192 + 2048)
        t_lo = at("t_lo", "wd0", [P, 2, PT], F32R, 8192 + 4096)
        mask = at("mask_t", "mask", [P, PT])
        wd_in = at("wd_in", "by", [P, 4, FQ])
        wd_tr = at("wd_tr", "by", [P, FT, P], F32, 4 * FQ * 4)
        part = (FT - 1) * P * 4
        wd_hi = [at(f"wd_hi{s}", p, [P, FT - 1, P], F32R) for s, p in enumerate(("wd0", "wring"))]
        wd_lo = [at(f"wd_lo{s}", p, [P, FT - 1, P], F32R, part) for s, p in enumerate(("wd0", "wring"))]
        wl_hi = [at(f"wl_hi{s}", p, [P, PAIRS, P], F32R, 2 * part) for s, p in enumerate(("wd0", "wring"))]
        wl_lo = [at(f"wl_lo{s}", p, [P, PAIRS, P], F32R, 2 * part + PAIRS * P * 4)
                 for s, p in enumerate(("wd0", "wring"))]
        td_a = at("td_a", "wy", [P, HALF])
        td_b = at("td_b", "wy", [P, HALF], F32, HALF * 4)
        wq_int = at("wq_int", "temps", [P, 16, P], I32)
        wq_val = at("wq_val", "temps", [P, 16, P], F32)
        wq_tr = at("wq_tr", "wy", [P, 2, H])
        wq_hi = at("wq_hi", "tstack", [P, KT, H], F32R)
        wq_lo = at("wq_lo", "sring", [P, KT, H], F32R)
        scale_t = at("scale_t", "sz", [P, 16])
        zero_t = at("zero_t", "sz", [P, 16], F32, 64)
        bias_t = at("bias_t", "bhl", [P, H])
        res = at("res", "wx", [P, 4, H])

        def bank(name):
            return ctx.enter_context(nc.psum_tensor(name, [P, HALF], F32))

        gate_ps = [bank(f"gate_ps{h}") for h in range(2)]
        up_ps = [bank(f"up_ps{h}") for h in range(2)]
        td_ps = [bank(f"td_ps{h}") for h in range(2)]
        down_ps = [bank(f"down_ps{h}") for h in range(2)]
        a_ps = td_ps
        t_ps = down_ps
        y_ps = gate_ps + up_ps

        def sem(name):
            return ctx.enter_context(nc.semaphore(name))

        x_landed = [sem(f"x_landed{c}") for c in range(4)]
        w_landed = [sem(f"w_landed{s}") for s in range(2)]
        a_landed, b_landed, ad_landed, bd_landed = (sem(n + "_landed") for n in ("a", "b", "ad", "bd"))
        stack_landed = [sem(f"stack_landed{s}") for s in range(2)]
        t_landed = [sem(f"t_landed{h}") for h in range(2)]
        wd_landed, wq_landed, sz_landed, bias_landed = (sem(n) for n in ("wd_l", "wq_l", "sz_l", "bias_l"))
        res_landed = [sem(f"res_landed{s}") for s in range(4)]
        out_stored = [sem(f"out_stored{s}") for s in range(4)]
        consts = sem("consts")
        mask_made = sem("mask_made")
        x_tred, x_hied, x_loed = sem("x_tred"), sem("x_hied"), sem("x_loed")
        a_permuted = sem("a_permuted")
        a_tred, a_hied, a_loed = sem("a_tred"), sem("a_hied"), sem("a_loed")
        w_tred, w_hied, w_loed = sem("w_tred"), sem("w_hied"), sem("w_loed")
        b_tred, b_hied, b_loed = sem("b_tred"), sem("b_hied"), sem("b_loed")
        ad_tred, ad_hied, ad_loed = sem("ad_tred"), sem("ad_hied"), sem("ad_loed")
        bd_tred = sem("bd_tred")
        t_done, t_hied, t_loed = sem("t_done"), sem("t_hied"), sem("t_loed")
        bank_read = sem("bank_read")
        unit_done = sem("unit_done")
        silu_done, act_done, act_hied, act_loed = (sem(n) for n in ("silu_done", "act_done", "act_hied", "act_loed"))
        td_used = sem("td_used")
        td_done, td_copied, td_summed, td_masked, td_hied, td_loed = (
            sem(n) for n in ("td_done", "td_copied", "td_summed", "td_masked", "td_hied", "td_loed"))
        wd_tred, wd_hied, wd_loed = sem("wd_tred"), sem("wd_hied"), sem("wd_loed")
        down_done, down_hied = sem("down_done"), sem("down_hied")
        wq_zeroed, wq_scaled = sem("wq_zeroed"), sem("wq_scaled")
        wq_tred, wq_hied, wq_loed = sem("wq_tred"), sem("wq_hied"), sem("wq_loed")
        biased = sem("biased")
        y_done, y_added = sem("y_done"), sem("y_added")

        block = ctx.enter_context(nc.Block())

        W_DMAS = 2 * 4 * 2
        W_LAST_DMAS = 2 * 4
        STACK_DMAS = PAIRS * 3
        T_DMAS = 2 * 2 * 3

        def peeled(j):
            return j, j // 2 + 1, j % 2

        def in_loop(i, step):
            return i * 2 + PROLOGUE_TILES + step, i + 2 + step // 2, step % 2

        ROUNDS = (FT - 1 - PROLOGUE_TILES) // 2

        @block.sync
        def _(sp):
            def load_x(c):
                rows = x_flat[c * PT:(c + 1) * PT, :].rearrange("(b r) (q c) -> q r b c", r=Q, q=4)
                for q in range(4):
                    sp.dma_start(x_in[q * Q:(q + 1) * Q, c * 8:(c + 1) * 8, :], rows[q]).then_inc(x_landed[c], 16)

            def load_w(j, slot, last=False):
                for g in range(2):
                    three = gu_w[g][0:F3, :].rearrange("(a r j) (q c) -> q r a j c", a=3, r=Q, q=4)
                    four = gu_w[g][F3:F, :].rearrange("(r j) (q c) -> q r j c", r=Q, q=4)
                    for q in range(4):
                        rows = slice(q * Q, (q + 1) * Q)
                        sp.dma_start(w_in[rows, slot, g, 0:3, :], three[q, :, :, j, :]).then_inc(w_landed[slot], 16)
                        if not last:
                            sp.dma_start(w_in[rows, slot, g, 3, :], four[q, :, j, :]).then_inc(w_landed[slot], 16)

            def move_stack(tile):
                j, use, slot = tile
                sp.wait_ge(b_loed, j + 1)
                for p in range(PAIRS):
                    for s, src in enumerate((b_hi, b_hi, b_lo)):
                        sp.dma_start(b_stack[s * Q:(s + 1) * Q, slot, p, :, :].bitcast(F32),
                                     src[p * Q:(p + 1) * Q, :, :].bitcast(F32)).then_inc(stack_landed[slot], 16)

            def move_t(h):
                sp.wait_ge(t_loed, h + 1)
                for p in range(2):
                    for g in range(2):
                        for s, src in enumerate((t_hi, t_lo, t_hi)):
                            rows = slice((2 * p + g) * Q, (2 * p + g + 1) * Q)
                            cols = slice(h * HALF + p * PT, h * HALF + (p + 1) * PT)
                            sp.dma_start(t_stack[s * Q:(s + 1) * Q, g, cols].bitcast(F32),
                                         src[rows, h, :].bitcast(F32)).then_inc(t_landed[h], 16)

            load_x(0)
            load_w(0, 0)
            load_x(1)
            load_x(2)
            load_x(3)
            load_w(1, 1)
            ids = [sp.value_load(idx_row[0:1, b:b + 1], min_val=0, max_val=R - 1) for b in range(NB)]
            for b in range(NB):
                rows = slice(b % 2 * R, b % 2 * R + R)
                for q in range(4):
                    n = FQ if q < 3 else LAST
                    sp.dma_start(ad_in[q * Q + b % 2 * R:q * Q + b % 2 * R + R, b // 2, 0:n],
                                 a_down[0, ids[b], :, q * FQ:q * FQ + n]).then_inc(ad_landed, 16)
            move_t(0)
            move_stack(peeled(0))
            move_t(1)
            for b in range(NB):
                sp.dma_start(bd_in[3 * Q:P, b // 2, b % 2, :, :],
                             b_down[0, ids[b]].rearrange("(q r t) c -> r q (t c)", q=4, r=Q)).then_inc(bd_landed, 16)
            for q in range(4):
                for src, dst in ((scale, scale_t), (zero_point, zero_t)):
                    sp.dma_start(dst[q * Q:(q + 1) * Q, :], src.rearrange("(b r) g -> g r b", r=Q)[q],
                                 allow_slow_non_contiguous=True).then_inc(sz_landed, 16)

            def period(tile, after):
                j, use, slot = tile
                sp.wait_ge(w_tred, j * 2 + 2)
                load_w(j + 2, slot)
                move_stack(after)

            for j in range(PROLOGUE_TILES):
                period(peeled(j), peeled(j + 1))
            with sp.Fori(0, ROUNDS - 1) as i:
                for step in range(2):
                    period(in_loop(i, step), in_loop(i, step + 1))
            period_j = FT - 3
            sp.wait_ge(w_tred, 2 * period_j + 2)
            load_w(FT - 1, period_j % 2, last=True)
            move_stack(peeled(FT - 2))
            move_stack(peeled(FT - 1))

            def load_wd(t):
                wd_rows = w_down.rearrange("(q r t) f -> t r q f", q=4, r=Q)[t]
                if t:
                    sp.wait_ge(wd_tred, t)
                for q in range(4):
                    n = FQ if q < 3 else LAST
                    sp.dma_start(wd_in[q * Q:(q + 1) * Q, :, 0:n],
                                 wd_rows[:, :, q * FQ:q * FQ + n]).then_inc(wd_landed, 16)

            load_wd(0)
            load_wd(1)
            sp.wait_ge(act_loed, 2 * FT)
            for q in range(4):
                sp.dma_start(wq_int[q * Q:(q + 1) * Q, :, :],
                             wq.rearrange("(b r) (q c) -> q r b c", r=Q, q=4)[q]).then_inc(wq_landed, 16)
            sp.dma_start(bias_t[:, :], bias.rearrange("(a n) -> a n", a=1).broadcast_to([P, H])).then_inc(bias_landed, 16)

            def load_res(n):
                if n >= 4:
                    sp.wait_ge(out_stored[n % 4], 16 * (n // 4))
                sp.dma_start(res[:, n % 4, :], x_flat[n * P:(n + 1) * P, :]).then_inc(res_landed[n % 4], 16)

            for n in range(4):
                load_res(n)
            load_wd(2)
            load_wd(3)
            for n in range(NB):
                sp.wait_ge(y_added, n + 1)
                sp.dma_start(out_flat[n * P:(n + 1) * P, :], res[:, n % 4, :]).then_inc(out_stored[n % 4], 16)
                if n + 4 < NB:
                    load_res(n + 4)
            for s in range(4):
                sp.wait_ge(out_stored[s], 16 * (NB // 4))

        @block.gpsimd
        def _(pool):
            nc.gpsimd.memset(ident[:, :], 0.0).then_inc(consts, 1)
            nc.gpsimd.memset(mask[0:Q, :], LORA_SCALE).then_inc(consts, 1)
            pool.wait_ge(consts, 2)
            nc.gpsimd.affine_select(out=ident[:, :], in_=ident[:, :], compare_op=ALU.not_equal, fill=1.0, base=0,
                                    pattern=[[-1, P]], channel_multiplier=1).then_inc(consts, 1)
            nc.gpsimd.affine_select(out=mask[0:Q, 0:T], in_=mask[0:Q, 0:T], compare_op=ALU.is_ge, fill=0.0,
                                    base=R - 1, pattern=[[0, T]], channel_multiplier=-1).then_inc(consts, 1)
            nc.gpsimd.affine_select(out=mask[0:Q, T:PT], in_=mask[0:Q, T:PT], compare_op=ALU.is_ge, fill=0.0,
                                    base=-R, pattern=[[0, T]], channel_multiplier=1).then_inc(consts, 1)
            pool.wait_ge(bias_landed, 16)
            for n in range(NB):
                pool.wait_ge(res_landed[n % 4], 16 * (n // 4 + 1))
                nc.gpsimd.tensor_tensor(res[:, n % 4, :], res[:, n % 4, :], bias_t[:, :], ALU.add).then_inc(biased, 1)

        @block.scalar
        def _(act):
            ids = [act.value_load(idx_row[0:1, b:b + 1], min_val=0, max_val=R - 1) for b in range(NB)]
            for g in range(2):
                for b in range(NB):
                    act.dma_start(a_in[b * R:(b + 1) * R, g, :], gu_a[g][0, ids[b]]).then_inc(a_landed, 16)
            for b in range(NB):
                rows = slice(b // 2 * Q, (b // 2 + 1) * Q)
                for g in range(2):
                    src = gu_b[g][0, ids[b]]
                    act.dma_start(b_in[rows, g, b % 2, 0:3 * FT * R].rearrange("p (q c) -> p q c", q=3),
                                  src[0:F3, :].rearrange("(q r j) c -> r q (j c)", q=3, r=Q)).then_inc(b_landed, 16)
                    act.dma_start(b_in[rows, g, b % 2, 3 * FT * R:FB * R],
                                  src[F3:F, :].rearrange("(r j) c -> r (j c)", r=Q)).then_inc(b_landed, 16)

            def x_part(c):
                act.wait_ge(x_tred, c + 1)
                cols = slice(c * PT, (c + 1) * PT)
                nc.scalar.copy(xt_hi[:, :, cols], x_tr[:, :, cols]).then_inc(x_hied, 1)

            def w_part(tile, quads=4):
                j, use, slot = tile
                for g in range(2):
                    act.wait_ge(w_tred, j * 2 + (g + 1))
                    nc.scalar.copy(w_hi[:, slot, g, :, 0:quads * Q], w_tr[:, g, :, 0:quads * Q]).then_inc(w_hied, 1)

            def b_part(j, quads=4):
                src = b_tr[:, :, :].rearrange("p g (q j r) -> p g q j r", q=4, j=FT) if quads == 4 else None
                if quads == 4:
                    src = src[:, :, :, j, :]
                    for g in range(2):
                        last = nc.scalar.copy(b_hi[:, g, :].rearrange("p (q r) -> p q r", q=4), src[:, g])
                else:
                    src = b_tr[:, :, 0:F3].rearrange("p g (q j r) -> p g q j r", q=3, j=FT)[:, :, :, j, :]
                    for g in range(2):
                        last = nc.scalar.copy(b_hi[:, g, 0:KL].rearrange("p (q r) -> p q r", q=3), src[:, g])
                last.then_inc(b_hied, 1)

            def ad_part(j, slot, rows=P):
                last = nc.scalar.copy(ad_parts[0:rows, slot, :, :, 0, :],
                                      ad_tr[0:rows, :, j, :].rearrange("p (h a) r -> p h a r", h=2))
                last.then_inc(ad_hied, 1)

            def evacuate(j):
                for h in range(2):
                    act.wait_ge(unit_done, j * 2 + (h + 1))
                    nc.scalar.activation(silu[:, h, :], gate_ps[h][:, :], ACT.Silu).then_inc(silu_done, 1)
                    act.wait_ge(act_done, j * 2 + (h + 1))
                    nc.scalar.copy(act_hi[:, j, h * HALF:(h + 1) * HALF], actf[:, h, :]).then_inc(act_hied, 1)

            def evacuate_last():
                j = FT - 1
                for h in range(2):
                    act.wait_ge(unit_done, 2 * j + h + 1)
                    nc.scalar.activation(silu[0:KL, h, :], gate_ps[h][0:KL, :], ACT.Silu).then_inc(silu_done, 1)
                    act.wait_ge(act_done, 2 * j + h + 1)
                    nc.scalar.copy(act_hi[0:KL, j, h * HALF:(h + 1) * HALF], actf[0:KL, h, :]).then_inc(act_hied, 1)

            act.wait_ge(a_landed, 2 * NB * 16)
            for g in range(2):
                nc.scalar.copy(a_perm[:, g, :, :].rearrange("p k (q r) -> p q k r", q=4),
                               a_in[:, g, :].rearrange("p (q k r) -> p q k r", q=4, k=KT)).then_inc(a_permuted, 1)
            x_part(0)
            x_part(1)
            w_part(peeled(0))
            for g in range(2):
                act.wait_ge(a_tred, g + 1)
                nc.scalar.copy(a_hi[:, :, :, g, :],
                               a_ps[g][:, :].rearrange("p (k a c) -> p k a c", k=KT, a=PAIRS)).then_inc(a_hied, 1)
            act.wait_ge(bank_read, 1)
            nc.scalar.copy(t_hi[:, 0, :], t_val[:, 0, :]).then_inc(t_hied, 1)
            act.wait_ge(b_tred, 2)
            b_part(0)
            x_part(2)
            x_part(3)
            act.wait_ge(bank_read, 2)
            nc.scalar.copy(t_hi[:, 1, :], t_val[:, 1, :]).then_inc(t_hied, 1)
            act.wait_ge(ad_tred, 1)

            def period(tile, after, quads=4):
                j, use, slot = tile
                nj, nuse, nslot = after
                if not isinstance(j, int) or j >= 2:
                    act.wait_ge(td_used, j - 1)
                ad_part(j, slot)
                if not isinstance(j, int) or j >= 1:
                    act.wait_ge(unit_done, j * 2)
                w_part(after, quads)
                act.wait_ge(stack_landed[slot], use * (16 * STACK_DMAS))
                b_part(nj, quads)
                evacuate(j)

            for j in range(PROLOGUE_TILES):
                period(peeled(j), peeled(j + 1))
            with act.Fori(0, ROUNDS - 1) as i:
                for step in range(2):
                    period(in_loop(i, step), in_loop(i, step + 1))
            period(peeled(FT - 3), peeled(FT - 2))
            period(peeled(FT - 2), peeled(FT - 1), 3)

            def wd_part(t):
                act.wait_ge(wd_tred, t + 1)
                s = t % 2
                nc.scalar.copy(wl_hi[s][3 * Q:P, :, :], bd_tr[3 * Q:P, :, t, :])
                nc.scalar.copy(wl_hi[s][0:KL, :, :],
                               wd_tr[0:KL, FT - 1:FT, :].broadcast_to([KL, PAIRS, P]))
                nc.scalar.copy(wd_hi[s][:, :, :], wd_tr[:, 0:FT - 1, :]).then_inc(wd_hied, 1)

            act.wait_ge(td_used, FT - 2)
            ad_part(FT - 1, (FT - 1) % 2, KL)
            wd_part(0)
            evacuate_last()
            for h in range(2):
                act.wait_ge(td_done, h + 1)
                if h:
                    act.wait_ge(td_loed, 1)
                for p in range(2):
                    cols = slice(p * PT, (p + 1) * PT)
                    nc.scalar.copy(td_a[3 * Q:P, cols], td_ps[h][2 * p * Q:(2 * p + 1) * Q, cols])
                    last = nc.scalar.copy(td_b[3 * Q:P, cols], td_ps[h][(2 * p + 1) * Q:(2 * p + 2) * Q, cols])
                last.then_inc(td_copied, 1)
                act.wait_ge(td_masked, h + 1)
                nc.scalar.copy(act_hi[3 * Q:P, FT - 1, h * HALF:(h + 1) * HALF], td_a[3 * Q:P, :]).then_inc(td_hied, 1)

            def down_part(t):
                for h in range(2):
                    act.wait_ge(down_done, 2 * t + h + 1)
                    nc.scalar.copy(dt_hi[:, t, h * HALF:(h + 1) * HALF], down_ps[h][:, :]).then_inc(down_hied, 1)

            for t in range(KT - 1):
                wd_part(t + 1)
                down_part(t)
            for t in range(KT):
                act.wait_ge(wq_tred, t + 1)
                nc.scalar.copy(wq_hi[:, t, :], wq_tr[:, t % 2, :]).then_inc(wq_hied, 1)
            down_part(KT - 1)

        @block.vector
        def _(dve):
            SUB = ALU.subtract

            def x_transpose(c):
                dve.wait_ge(x_landed[c], 4 * 16)
                for k in range(KT):
                    last = nc.vector.transpose(x_tr[:, k, c * PT:(c + 1) * PT].rearrange("p (b r) -> p b r", r=Q),
                                               x_in[:, c * 8:(c + 1) * 8, k * Q:(k + 1) * Q])
                last.then_inc(x_tred, 1)

            def x_part(c):
                dve.wait_ge(x_hied, c + 1)
                cols = slice(c * PT, (c + 1) * PT)
                nc.vector.tensor_tensor(xt_lo[:, :, cols], x_tr[:, :, cols], xt_hi[:, :, cols].bitcast(F32),
                                        SUB).then_inc(x_loed, 1)

            def w_transpose(tile, quads=4):
                j, use, slot = tile
                dve.wait_ge(w_landed[slot], use * (16 * W_DMAS) if quads == 4
                            else (use - 1) * 16 * W_DMAS + 16 * W_LAST_DMAS)
                for g in range(2):
                    nc.vector.transpose(
                        w_tr[:, g, :, 0:quads * Q].rearrange("p k (a r) -> p a k r", r=Q),
                        w_in[:, slot, g, 0:quads, :].rearrange("p a (k r) -> p a k r", r=Q)).then_inc(w_tred, 1)

            def w_part(tile, quads=4):
                j, use, slot = tile
                for g in range(2):
                    dve.wait_ge(w_hied, j * 2 + (g + 1))
                    m = quads * Q
                    nc.vector.tensor_tensor(w_lo[:, slot, g, :, 0:m], w_tr[:, g, :, 0:m],
                                            w_hi[:, slot, g, :, 0:m].bitcast(F32), SUB).then_inc(w_loed, 1)

            def b_part(j, quads=4):
                dve.wait_ge(b_hied, j + 1)
                m = quads * Q
                for g in range(2):
                    src = b_tr[:, g, 0:quads * FQ].rearrange("p (q j r) -> p q j r", q=quads, j=FT)[:, :, j, :]
                    last = nc.vector.tensor_tensor(b_lo[:, g, 0:m].rearrange("p (q r) -> p q r", q=quads), src,
                                                   b_hi[:, g, 0:m].rearrange("p (q r) -> p q r", q=quads).bitcast(F32),
                                                   SUB)
                last.then_inc(b_loed, 1)

            def ad_part(j, slot, rows=P):
                dve.wait_ge(ad_hied, j + 1)
                nc.vector.tensor_tensor(ad_parts[0:rows, slot, :, :, 1, :],
                                        ad_tr[0:rows, :, j, :].rearrange("p (h a) r -> p h a r", h=2),
                                        ad_parts[0:rows, slot, :, :, 0, :].bitcast(F32), SUB).then_inc(ad_loed, 1)

            def evacuate(j, rows=P):
                for h in range(2):
                    dve.wait_ge(silu_done, j * 2 + (h + 1))
                    nc.vector.tensor_tensor(actf[0:rows, h, :], up_ps[h][0:rows, :], silu[0:rows, h, :],
                                            ALU.mult).then_inc(act_done, 1)
                    dve.wait_ge(act_hied, j * 2 + (h + 1))
                    cols = slice(h * HALF, (h + 1) * HALF)
                    nc.vector.tensor_tensor(act_lo[0:rows, j, cols], actf[0:rows, h, :],
                                            act_hi[0:rows, j, cols].bitcast(F32), SUB).then_inc(act_loed, 1)

            def t_mask(h):
                dve.wait_ge(t_done, h + 1)
                for p in range(2):
                    rows = slice(2 * p * Q, 2 * (p + 1) * Q)
                    last = nc.vector.tensor_tensor(t_val[rows, h, :], t_ps[h][rows, p * PT:(p + 1) * PT],
                                                   mask[rows, :], ALU.mult)
                last.then_inc(bank_read, 1)

            def t_part(h):
                dve.wait_ge(t_hied, h + 1)
                nc.vector.tensor_tensor(t_lo[:, h, :], t_val[:, h, :], t_hi[:, h, :].bitcast(F32),
                                        SUB).then_inc(t_loed, 1)

            x_transpose(0)
            w_transpose(peeled(0))
            x_transpose(1)
            x_part(0)
            w_part(peeled(0))
            x_part(1)
            for g in range(2):
                dve.wait_ge(a_hied, g + 1)
                nc.vector.tensor_tensor(a_lo[:, :, :, g, :],
                                        a_ps[g][:, :].rearrange("p (k a c) -> p k a c", k=KT, a=PAIRS),
                                        a_hi[:, :, :, g, :].bitcast(F32), SUB).then_inc(a_loed, 1)
            dve.wait_ge(consts, 5)
            for q in range(1, 4):
                last = nc.vector.tensor_copy(mask[q * Q:(q + 1) * Q, :], mask[0:Q, :])
            last.then_inc(mask_made, 1)
            dve.wait_ge(mask_made, 1)
            dve.wait_ge(b_landed, NB * 2 * 2 * 16)
            for g in range(2):
                nc.vector.transpose(b_tr[:, g, 0:F].rearrange("p (b r) -> p b r", r=Q),
                                    b_in[:, g, :, :].rearrange("p e (b c) -> p b e c", c=R)).then_inc(b_tred, 1)
            t_mask(0)
            t_part(0)
            b_part(0)
            for c in (2, 3):
                x_transpose(c)
            for c in (2, 3):
                x_part(c)
            t_mask(1)
            t_part(1)
            dve.wait_ge(ad_landed, NB * 4 * 16)
            for a in range(PAIRS):
                nc.vector.transpose(ad_tr[0:KL, a, :, :], ad_in[0:KL, a, :].rearrange("p (r j) -> p j r", j=FT))
                last = nc.vector.transpose(ad_tr[KL:P, a, 0:NL, :],
                                           ad_in[KL:P, a, 0:LAST].rearrange("p (r j) -> p j r", j=NL))
            last.then_inc(ad_tred, 1)

            def period(tile, after, quads=4):
                j, use, slot = tile
                ad_part(j, slot)
                w_transpose(after, quads)
                w_part(after, quads)
                b_part(after[0], quads)
                evacuate(j)

            period(peeled(0), peeled(1))
            dve.wait_ge(bd_landed, NB * 16)
            dve.wait_ge(t_landed[1], 16 * T_DMAS)
            for a in range(PAIRS):
                for t in range(KT):
                    last = nc.vector.transpose(
                        bd_tr[KL:P, a, t, :].rearrange("p (q r) -> p q r", q=4),
                        bd_in[KL:P, a, :, :, t * R:(t + 1) * R].rearrange("p e q c -> p q e c"))
            last.then_inc(bd_tred, 1)
            period(peeled(1), peeled(2))
            with dve.Fori(0, ROUNDS - 1) as i:
                for step in range(2):
                    period(in_loop(i, step), in_loop(i, step + 1))
            period(peeled(FT - 3), peeled(FT - 2))
            period(peeled(FT - 2), peeled(FT - 1), 3)

            def wd_transpose(t):
                dve.wait_ge(wd_landed, (t + 1) * 4 * 16)
                if t:
                    dve.wait_ge(wd_loed, t)
                if t == 1:
                    dve.wait_ge(unit_done, 2 * FT)
                if t >= 2:
                    dve.wait_ge(down_done, 2 * (t - 1))
                for q in range(4):
                    cols = slice(q * Q, (q + 1) * Q)
                    nc.vector.transpose(wd_tr[0:KL, :, cols], wd_in[0:KL, q, :].rearrange("p (r j) -> p j r", j=FT))
                    last = nc.vector.transpose(wd_tr[KL:P, 0:NL, cols],
                                               wd_in[KL:P, q, 0:LAST].rearrange("p (r j) -> p j r", j=NL))
                last.then_inc(wd_tred, 1)

            def wd_part(t):
                s = t % 2
                dve.wait_ge(wd_hied, t + 1)
                nc.vector.tensor_tensor(wl_lo[s][KL:P, :, :], bd_tr[KL:P, :, t, :],
                                        wl_hi[s][KL:P, :, :].bitcast(F32), SUB)
                nc.vector.tensor_tensor(wl_lo[s][0:KL, :, :], wd_tr[0:KL, FT - 1:FT, :].broadcast_to([KL, PAIRS, P]),
                                        wl_hi[s][0:KL, :, :].bitcast(F32), SUB)
                nc.vector.tensor_tensor(wd_lo[s][:, :, :], wd_tr[:, 0:FT - 1, :], wd_hi[s][:, :, :].bitcast(F32),
                                        SUB).then_inc(wd_loed, 1)

            ad_part(FT - 1, (FT - 1) % 2, KL)
            wd_transpose(0)
            wd_part(0)
            evacuate(FT - 1, KL)
            for h in range(2):
                dve.wait_ge(td_copied, h + 1)
                nc.vector.tensor_tensor(td_a[KL:P, :], td_a[KL:P, :], td_b[KL:P, :], ALU.add).then_inc(td_summed, 1)
                dve.wait_ge(td_summed, h + 1)
                for p in range(2):
                    cols = slice(p * PT, (p + 1) * PT)
                    last = nc.vector.tensor_tensor(td_a[KL:P, cols], td_a[KL:P, cols], mask[KL:P, :], ALU.mult)
                last.then_inc(td_masked, 1)
                dve.wait_ge(td_hied, h + 1)
                cols = slice(h * HALF, (h + 1) * HALF)
                nc.vector.tensor_tensor(act_lo[KL:P, FT - 1, cols], td_a[KL:P, :],
                                        act_hi[KL:P, FT - 1, cols].bitcast(F32), SUB).then_inc(td_loed, 1)

            def down_part(t):
                for h in range(2):
                    dve.wait_ge(down_hied, 2 * t + h + 1)
                    cols = slice(h * HALF, (h + 1) * HALF)
                    nc.vector.tensor_tensor(dt_lo[:, t, cols], down_ps[h][:, :], dt_hi[:, t, cols].bitcast(F32),
                                            SUB).then_inc(bank_read, 1)

            for t in range(KT - 1):
                wd_transpose(t + 1)
                wd_part(t + 1)
                if t == KT - 2:
                    dve.wait_ge(wq_landed, 4 * 16)
                    dve.wait_ge(sz_landed, 2 * 4 * 16)
                    nc.vector.tensor_tensor(wq_val[:, :, :], wq_int[:, :, :],
                                            zero_t[:, :].unsqueeze(2).broadcast_to([P, 16, P]), SUB).then_inc(wq_zeroed, 1)
                    dve.wait_ge(wq_zeroed, 1)
                    nc.vector.tensor_tensor(wq_val[:, :, :], wq_val[:, :, :],
                                            scale_t[:, :].unsqueeze(2).broadcast_to([P, 16, P]), ALU.mult).then_inc(wq_scaled, 1)
                down_part(t)
            dve.wait_ge(wq_scaled, 1)
            for t in range(KT):
                nc.vector.transpose(wq_tr[:, t % 2, :].rearrange("p (b r) -> p b r", r=Q),
                                    wq_val[:, :, :].rearrange("p b (r t) -> p b r t", t=KT)[:, :, :, t]).then_inc(wq_tred, 1)
                dve.wait_ge(wq_hied, t + 1)
                nc.vector.tensor_tensor(wq_lo[:, t, :], wq_tr[:, t % 2, :], wq_hi[:, t, :].bitcast(F32),
                                        SUB).then_inc(wq_loed, 1)
            down_part(KT - 1)
            for n in range(NB):
                dve.wait_ge(y_done, n + 1)
                dve.wait_ge(biased, n + 1)
                nc.vector.tensor_tensor(res[:, n % 4, :], y_ps[n % 4][:, :], res[:, n % 4, :], ALU.add).then_inc(y_added, 1)

        @block.tensor
        def _(pe):
            mm = nc.tensor.matmul

            def project_t(h):
                pe.wait_ge(x_hied, 2 * h + 2)
                pe.wait_ge(x_loed, 2 * h + 2)
                if h == 0:
                    pe.wait_ge(a_hied, 2)
                    pe.wait_ge(a_loed, 2)
                cols = slice(h * HALF, (h + 1) * HALF)
                n = 0
                for w, v in ((a_hi, xt_hi), (a_hi, xt_lo), (a_lo, xt_hi)):
                    for k in range(KT):
                        last = mm(t_ps[h][:, :], w[:, k, 2 * h:2 * h + 2, :, :], v[:, k, cols],
                                  start=n == 0, stop=n == 3 * KT - 1)
                        n += 1
                last.then_inc(t_done, 1)

            def gate_up(tile, h, m=P):
                j, use, slot = tile
                if not isinstance(j, int) or j > 0:
                    pe.wait_ge(act_done, j * 2 + (h - 1))
                else:
                    pe.wait_ge(a_loed, 2)
                cols = slice(h * HALF, (h + 1) * HALF)
                banks = (gate_ps[h], up_ps[h])
                products = [(w, v, k) for w, v in ((w_hi, xt_hi), (w_hi, xt_lo), (w_lo, xt_hi)) for k in range(KT)]
                for g in range(2):
                    pe.wait_ge(w_hied, j * 2 + (g + 1))
                    for n, (w, v, k) in enumerate(products[:-1]):
                        if n == 2 * KT:
                            pe.wait_ge(w_loed, j * 2 + (g + 1))
                        mm(banks[g][0:m, :], w[:, slot, g, k, 0:m], v[:, k, cols], start=n == 0, stop=False)
                pe.wait_ge(stack_landed[slot], use * (16 * STACK_DMAS))
                pe.wait_ge(t_landed[h], 16 * T_DMAS)
                w, v, k = products[-1]
                for g in range(2):
                    for p in range(2):
                        toks = slice(h * HALF + p * PT, h * HALF + (p + 1) * PT)
                        mm(banks[g][0:m, p * PT:(p + 1) * PT], b_stack[0:KL, slot, 2 * h + p, g, 0:m],
                           t_stack[0:KL, g, toks], start=False, stop=False, skip_group_check=True)
                    last = mm(banks[g][0:m, :], w[:, slot, g, k, 0:m], v[:, k, cols], start=False, stop=True)
                last.then_inc(unit_done, 1)

            def project_act(j, slot, h, rows=P, first=False, last_tile=False):
                pe.wait_ge(act_loed, j * 2 + (h + 1))
                pe.wait_ge(ad_loed, j + 1)
                cols = slice(h * HALF, (h + 1) * HALF)
                w = ad_parts[0:rows, slot, h, :, :, :]
                mm(td_ps[h][:, :], w, act_hi[0:rows, j, cols], start=first, stop=False, skip_group_check=True)
                last = mm(td_ps[h][:, :], w, act_lo[0:rows, j, cols], start=False, stop=last_tile,
                          skip_group_check=True)
                if last_tile:
                    last.then_inc(td_done, 1)
                elif h == 1:
                    last.then_inc(td_used, 1)

            pe.wait_ge(consts, 3)
            for g in range(2):
                pe.wait_ge(a_permuted, g + 1)
                for k in range(KT):
                    last = nc.tensor.transpose(
                        a_ps[g][:, k * P:(k + 1) * P],
                        a_perm[:, g, k, :], ident[:, :])
                last.then_inc(a_tred, 1)

            for h in range(2):
                project_t(h)
                gate_up(peeled(0), h)
            for h in range(2):
                gate_up(peeled(1), h)
                project_act(0, 0, h, first=True)
            with pe.Fori(0, ROUNDS) as i:
                for step in range(2):
                    tile = in_loop(i, step)
                    for h in range(2):
                        gate_up(tile, h)
                        project_act(i * 2 + (PROLOGUE_TILES + step - 1), (step + 1) % 2, h)
            for h in range(2):
                gate_up(peeled(FT - 1), h, KL)
                project_act(FT - 2, (FT - 2) % 2, h)
            for h in range(2):
                project_act(FT - 1, (FT - 1) % 2, h, rows=KL, last_tile=True)

            with pe.Fori(0, KT // 2) as i:
                for s in range(2):
                    for h in range(2):
                        group = i * 4 + (2 * s + h)
                        cols = slice(h * HALF, (h + 1) * HALF)
                        pe.wait_ge(wd_loed, i * 2 + (s + 1))
                        pe.wait_ge(bank_read, group + 1)
                        products = [(w, v, j) for w, v in ((wd_hi, act_hi), (wd_hi, act_lo), (wd_lo, act_hi))
                                    for j in range(FT - 1)]
                        for n, (w, v, j) in enumerate(products[:-1]):
                            mm(down_ps[h][:, :], w[s][:, j, :], v[:, j, cols], start=n == 0, stop=False)
                        pe.wait_ge(td_loed, h + 1)
                        for p in range(2):
                            toks = slice(h * HALF + p * PT, h * HALF + (p + 1) * PT)
                            for w, v in ((wl_hi, act_hi), (wl_hi, act_lo), (wl_lo, act_hi)):
                                mm(down_ps[h][:, p * PT:(p + 1) * PT], w[s][:, 2 * h + p, :],
                                   v[:, FT - 1, toks], start=False, stop=False, skip_group_check=True)
                        w, v, j = products[-1]
                        last = mm(down_ps[h][:, :], w[s][:, j, :], v[:, j, cols], start=False, stop=True)
                        last.then_inc(down_done, 1)

            pe.wait_ge(wq_loed, KT)
            for n in range(NB):
                pe.wait_ge(bank_read, 2 + 2 * KT - 1 + n // (NB // 2))
                if n >= 4:
                    pe.wait_ge(y_added, n - 3)
                toks = slice(n * P, (n + 1) * P)
                c = 0
                for v, w in ((dt_hi, wq_hi), (dt_hi, wq_lo), (dt_lo, wq_hi)):
                    for t in range(KT):
                        last = mm(y_ps[n % 4][:, :], v[:, t, toks], w[:, t, :], start=c == 0, stop=c == 3 * KT - 1)
                        c += 1
                last.then_inc(y_done, 1)


_INS = ['x', 'itok_B_2_6', 'L0_cond_W_gate', 'L0_cond_W_up', 'L0_cond_W_down', 'L0_cond_A_gate', 'L0_cond_B_gate',
        'L0_cond_A_up', 'L0_cond_B_up', 'L0_cond_A_down', 'L0_cond_B_down', 'L0_ffn_weight_q', 'L0_ffn_scale',
        'L0_ffn_zero_point', 'L0_ffn_bias']
_OUT = ((NB, T, H), 'float32')


def kernel(**inputs):
    import numpy as _np
    import concourse.bacc as _bacc
    from concourse import mybir as _mybir
    from concourse.bass_utils import run_bass_kernel_spmd as _run

    nc = _bacc.Bacc("TRN2", target_bir_lowering=False, num_devices=1)
    arrays, args = {}, []
    for name in _INS:
        a = _np.ascontiguousarray(inputs[name])
        arrays[f"in_{name}"] = a
        args.append(nc.dram_tensor(f"in_{name}", a.shape, _mybir.dt.from_np(a.dtype), kind="ExternalInput").ap())
    out = nc.dram_tensor("out_y", _OUT[0], _mybir.dt.from_np(_np.dtype(_OUT[1])), kind="ExternalOutput").ap()
    adaln_ffn(nc, *args, out)
    r = _run(nc, [arrays], core_ids=[0])
    return r.results[0]["out_y"]
```

```python
from contextlib import ExitStack

import concourse.bass as bass
from concourse import mybir

F32 = mybir.dt.float32
F32R = mybir.dt.float32r
I32 = mybir.dt.int32
ALU = mybir.AluOpType
ACT = mybir.ActivationFunctionType

P = 128
Q = 32
NB, T, H, F, R = 8, 128, 512, 1376, 16
NT = NB * T
HALF = NT // 2
KT = H // P
FB = F // Q
FT = -(-FB // 4)
FQ = FT * Q
F3 = 3 * FQ
LAST = F - F3
NL = LAST // Q
KL = 3 * Q
PAIRS = NB // 2
PT = 2 * T
LORA_SCALE = 0.5
PROLOGUE_TILES = 3


def adaln_ffn(nc, x, idx, w_gate, w_up, w_down, a_gate, b_gate, a_up, b_up, a_down, b_down,
              wq, scale, zero_point, bias, out):
    gu_w = (w_gate, w_up)
    gu_a = (a_gate, a_up)
    gu_b = (b_gate, b_up)
    x_flat = x.rearrange("b t h -> (b t) h")
    out_flat = out.rearrange("b t h -> (b t) h")
    idx_row = idx.rearrange("(a b) -> a b", a=1)

    with ExitStack() as ctx:
        size = 212736
        arena = ctx.enter_context(nc.sbuf_tensor("arena", [P, size // 4], F32))
        base = nc.sbuf_base - size
        base = (base + 31) // 32 * 32
        places = {}
        top = [0]

        def room(name, nbytes):
            places[name] = base + top[0]
            top[0] += nbytes
            assert top[0] <= size, (name, top[0])

        def at(name, place, shape, dt=F32, plus=0):
            return nc.alloc_sbuf_tensor_at(name, shape, dt, offset=places[place] + plus)

        room("tokens", 2 * KT * NT * 4)
        room("act", 2 * FT * NT * 4)
        room("wring", 2 * 2 * 2 * KT * P * 4)
        room("wx", 2 * 2 * KT * P * 4)
        room("wy", 2 * KT * P * 4)
        room("temps", 4 * HALF * 4)
        room("by", 2 * FQ * 4 * 4)
        room("bhl", 2 * 2 * P * 4)
        room("sring", 2 * PAIRS * 2 * P * 4)
        room("ady", PAIRS * FQ * 4)
        room("adring", 2 * 2 * P * 4)
        room("tstack", 2 * NT * 4)
        room("wd0", 2 * (FT - 1) * P * 4 + PAIRS * 2 * P * 4)
        room("mask", PT * 4)
        room("sz", 2 * 4 * KT * 4)

        xt_hi = at("xt_hi", "tokens", [P, KT, NT], F32R)
        xt_lo = at("xt_lo", "tokens", [P, KT, NT], F32R, KT * NT * 4)
        dt_hi = at("dt_hi", "tokens", [P, KT, NT], F32R)
        dt_lo = at("dt_lo", "tokens", [P, KT, NT], F32R, KT * NT * 4)
        act_hi = at("act_hi", "act", [P, FT, NT], F32R)
        act_lo = at("act_lo", "act", [P, FT, NT], F32R, FT * NT * 4)
        early = 2 * NT * 4
        x_in = at("x_in", "act", [P, NB, H], F32, early)
        a_in = at("a_in", "act", [P, 2, H], F32, early + 16384)
        w_first = at("w_first", "act", [P, 2, H], F32, early + 20480)
        ad_rows = at("ad_rows", "act", [P, F], F32, early + 24576)
        ident = at("ident", "act", [P, P], F32, early + 30208)
        idx_all = at("idx_all", "act", [P, NB], I32, early + 30720)
        row_off = at("row_off", "act", [P, NB], F32, early + 30752)
        own = at("own", "act", [P, NB], F32, early + 30784)
        row_all = at("row_all", "act", [P, NB], F32, early + 30816)
        row_own = at("row_own", "act", [P, NB], F32, early + 30848)
        row_sum = at("row_sum", "act", [P, 1], F32, early + 30912)
        row_id = at("row_id", "act", [P, 1], mybir.dt.uint32, early + 30880)
        low = FT * NT * 4 + early
        b_in = at("b_in", "act", [P, 2, 2, FB * R], F32, low)
        a_hi = at("a_hi", "act", [P, KT, PAIRS, 2, Q], F32R, low + 11264)
        a_lo = at("a_lo", "act", [P, KT, PAIRS, 2, Q], F32R, low + 11264 + 4096)
        ad_in = at("ad_in", "act", [P, PAIRS, FQ], F32, low + 11264 + 8192)
        w_in = at("w_in", "wx", [P, 2, 2, 4, P])
        w_tr = at("w_tr", "wy", [P, 2, KT, P])
        w_hi = at("w_hi", "wring", [P, 2, 2, KT, P], F32R)
        w_lo = at("w_lo", "wring", [P, 2, 2, KT, P], F32R, 2 * 2 * KT * P * 4)
        silu = at("silu", "temps", [P, 2, HALF])
        actf = at("actf", "temps", [P, 2, HALF], F32, 2 * HALF * 4)
        b_tr = at("b_tr", "by", [P, 2, 4 * FQ])
        b_hi = at("b_hi", "bhl", [P, 2, P], F32R)
        b_lo = at("b_lo", "bhl", [P, 2, P], F32R, 2 * P * 4)
        b_stack = at("b_stack", "sring", [P, 2, PAIRS, 2, P], F32R)
        ad_tr = at("ad_tr", "ady", [P, PAIRS, FT, Q])
        ad_parts = at("ad_parts", "adring", [P, 2, 2, 2, 2, Q], F32R)
        ad_tail = at("ad_tail", "sring", [P, 2, 2, 2, Q], F32R, PAIRS * 2 * P * 4)
        t_stack = at("t_stack", "tstack", [P, 2, NT], F32R)
        bd_tr = at("bd_tr", "tstack", [P, PAIRS, KT, P])
        bd_in = at("bd_in", "wd0", [P, PAIRS, 2, 4, KT * R])
        t_val = at("t_val", "wd0", [P, 2, PT], F32, 8192)
        t_hi = at("t_hi", "wd0", [P, 2, PT], F32R, 8192 + 2048)
        t_lo = at("t_lo", "wd0", [P, 2, PT], F32R, 8192 + 4096)
        mask = at("mask_t", "mask", [P, PT])
        wd_in = at("wd_in", "by", [P, 4, FQ])
        wd_tr = at("wd_tr", "by", [P, FT, P], F32, 4 * FQ * 4)
        part = (FT - 1) * P * 4
        wd_hi = [at(f"wd_hi{s}", p, [P, FT - 1, P], F32R) for s, p in enumerate(("wd0", "wring"))]
        wd_lo = [at(f"wd_lo{s}", p, [P, FT - 1, P], F32R, part) for s, p in enumerate(("wd0", "wring"))]
        wl_hi = [at(f"wl_hi{s}", p, [P, PAIRS, P], F32R, 2 * part) for s, p in enumerate(("wd0", "wring"))]
        wl_lo = [at(f"wl_lo{s}", p, [P, PAIRS, P], F32R, 2 * part + PAIRS * P * 4)
                 for s, p in enumerate(("wd0", "wring"))]
        td_a = [at(f"td_a{h}", p, [P, HALF]) for h, p in enumerate(("wy", "temps"))]
        td_b = [at(f"td_b{h}", p, [P, HALF], F32, HALF * 4) for h, p in enumerate(("wy", "temps"))]
        wq_int = at("wq_int", "temps", [P, 16, P], I32)
        wq_val = at("wq_val", "temps", [P, 16, P], F32)
        wq_tr = at("wq_tr", "wy", [P, 2, H])
        wq_hi = at("wq_hi", "tstack", [P, KT, H], F32R)
        wq_lo = at("wq_lo", "sring", [P, KT, H], F32R)
        scale_t = at("scale_t", "sz", [P, 16])
        zero_t = at("zero_t", "sz", [P, 16], F32, 64)
        bias_t = at("bias_t", "bhl", [P, H])
        res = at("res", "wx", [P, 4, H])

        def bank(name):
            return ctx.enter_context(nc.psum_tensor(name, [P, HALF], F32))

        gate_ps = [bank(f"gate_ps{h}") for h in range(2)]
        up_ps = [bank(f"up_ps{h}") for h in range(2)]
        td_ps = [bank(f"td_ps{h}") for h in range(2)]
        down_ps = [bank(f"down_ps{h}") for h in range(2)]
        x_ps = [gate_ps + up_ps, [gate_ps[1], up_ps[1]] + td_ps]
        w_ps = td_ps
        a_ps = down_ps
        t_ps = down_ps
        y_ps = gate_ps + up_ps

        def sem(name):
            return ctx.enter_context(nc.semaphore(name))

        x_landed = [sem(f"x_landed{c}") for c in range(4)]
        first_landed = [sem(f"first_landed{g}") for g in range(2)]
        w_landed = [sem(f"w_landed{s}") for s in range(2)]
        up_landed = [sem(f"up_landed{s}") for s in range(2)]
        a_landed = [sem(f"a_landed{g}") for g in range(2)]
        b_landed = sem("b_landed")
        b_up_landed = sem("b_up_landed")
        ad_landed, bd_landed = (sem(n + "_landed") for n in ("ad", "bd"))
        idx_landed = sem("idx_landed")
        rows_made = sem("rows_made")
        wd_landed, wq_landed, sz_landed, bias_landed = (sem(n) for n in ("wd_l", "wq_l", "sz_l", "bias_l"))
        res_landed = [sem(f"res_landed{s}") for s in range(4)]
        out_stored = [sem(f"out_stored{s}") for s in range(4)]
        consts = sem("consts")
        ident_made = sem("ident_made")
        mask_made = sem("mask_made")

        x_tred, x_hied, x_loed = sem("x_tred"), sem("x_hied"), sem("x_loed")
        scratch_set = sem("scratch_set")
        first_tred = sem("first_tred")
        stack_hied, stack_loed = sem("stack_hied"), sem("stack_loed")
        ts_hied, ts_loed = sem("ts_hied"), sem("ts_loed")
        a_tred, a_hied, a_loed = sem("a_tred"), sem("a_hied"), sem("a_loed")
        w_tred, w_hied, w_loed = sem("w_tred"), sem("w_hied"), sem("w_loed")
        ad_moved = sem("ad_moved")
        b_tred, b_hied, b_loed = sem("b_tred"), sem("b_hied"), sem("b_loed")
        ad_tred, ad_hied, ad_loed = sem("ad_tred"), sem("ad_hied"), sem("ad_loed")
        bd_tred = sem("bd_tred")
        t_done, t_hied, t_loed = sem("t_done"), sem("t_hied"), sem("t_loed")
        bank_read = sem("bank_read")
        unit_done = sem("unit_done")
        silu_done, act_done, act_hied, act_loed = (sem(n) for n in ("silu_done", "act_done", "act_hied", "act_loed"))
        td_used = sem("td_used")
        td_done, td_copied, td_summed, td_masked, td_hied, td_loed = (
            sem(n) for n in ("td_done", "td_copied", "td_summed", "td_masked", "td_hied", "td_loed"))
        wd_tred, wd_hied, wd_loed = sem("wd_tred"), sem("wd_hied"), sem("wd_loed")
        down_done, down_hied = sem("down_done"), sem("down_hied")
        wq_zeroed, wq_scaled = sem("wq_zeroed"), sem("wq_scaled")
        wq_tred, wq_hied, wq_loed = sem("wq_tred"), sem("wq_hied"), sem("wq_loed")
        biased = sem("biased")
        y_done, y_added = sem("y_done"), sem("y_added")

        block = ctx.enter_context(nc.Block())

        W_LOAD = 4 * 2 * 16
        W_LAST = 4 * 16
        B_LOAD = 2 * 16

        def peeled(j):
            return j, (j + 1) // 2, j % 2

        def in_loop(i, step):
            first = PROLOGUE_TILES + step
            return i * 2 + first, i + (first + 1) // 2, first % 2

        ROUNDS = (FT - 2 - PROLOGUE_TILES) // 2

        def load_w(eng, landed, g, j, slot, last=False):
            three = gu_w[g][0:F3, :].rearrange("(a r j) (q c) -> q r a j c", a=3, r=Q, q=4)
            four = gu_w[g][F3:F, :].rearrange("(r j) (q c) -> q r j c", r=Q, q=4)
            for q in range(4):
                rows = slice(q * Q, (q + 1) * Q)
                eng.dma_start(w_in[rows, slot, g, 0:3, :], three[q, :, :, j, :]).then_inc(landed[slot], 16)
                if not last:
                    eng.dma_start(w_in[rows, slot, g, 3, :], four[q, :, j, :]).then_inc(landed[slot], 16)

        def load_ids(eng):
            regs = [eng.alloc_register(f"adapter{b}") for b in range(NB)]
            for b in range(0, NB, 4):
                eng.load(regs[b:b + 4], idx_row[0:1, b:b + 4])
            return [eng.snap(reg, min_val=0, max_val=R - 1) for reg in regs]

        def load_b(eng, landed, g, batches, ids):
            for b in batches:
                rows = slice(b // 2 * Q, (b // 2 + 1) * Q)
                src = gu_b[g][0, ids[b]]
                eng.dma_start(b_in[rows, g, b % 2, 0:3 * FT * R].rearrange("p (q c) -> p q c", q=3),
                              src[0:F3, :].rearrange("(q r j) c -> r q (j c)", q=3, r=Q)).then_inc(landed, 16)
                eng.dma_start(b_in[rows, g, b % 2, 3 * FT * R:FB * R],
                              src[F3:F, :].rearrange("(r j) c -> r (j c)", r=Q)).then_inc(landed, 16)

        @block.sync
        def _(sp):
            def load_x(c):
                sp.dma_start(x_in[:, 2 * c:2 * c + 2, :], x[2 * c:2 * c + 2].rearrange("b t h -> t b h")
                             ).then_inc(x_landed[c], 16)

            def load_first(g):
                sp.dma_start(w_first[0:KL, g, :], gu_w[g][0:F3, :].rearrange("(m j) h -> m j h", j=FT)[:, 0, :]
                             ).then_inc(first_landed[g], 16)
                sp.dma_start(w_first[KL:P, g, :], gu_w[g][F3:F, :].rearrange("(m j) h -> m j h", j=NL)[:, 0, :]
                             ).then_inc(first_landed[g], 16)

            load_x(0)
            load_x(1)
            load_first(0)
            load_first(1)
            load_x(2)
            load_x(3)
            ids = load_ids(sp)
            load_b(sp, b_landed, 0, range(NB), ids)
            load_b(sp, b_landed, 1, range(NB // 2, NB), ids)
            load_w(sp, w_landed, 0, 1, 1)
            load_w(sp, w_landed, 0, 2, 0)
            load_w(sp, w_landed, 1, 2, 0)

            def period(tile):
                j, use, slot = tile
                sp.wait_ge(w_tred, j * 2)
                load_w(sp, w_landed, 0, j + 2, slot)

            for j in range(1, PROLOGUE_TILES):
                period(peeled(j))
            with sp.Fori(0, ROUNDS - 1) as i:
                for step in range(2):
                    period(in_loop(i, step))
            period(peeled(FT - 4))
            sp.wait_ge(w_tred, 2 * (FT - 3))
            load_w(sp, w_landed, 0, FT - 1, (FT - 1) % 2, last=True)
            sp.wait_ge(b_loed, FT)
            sp.wait_ge(stack_hied, FT)

            def load_wd(t):
                wd_rows = w_down.rearrange("(q r t) f -> t r q f", q=4, r=Q)[t]
                if t:
                    sp.wait_ge(wd_tred, t)
                for q in range(4):
                    n = FQ if q < 3 else LAST
                    sp.dma_start(wd_in[q * Q:(q + 1) * Q, :, 0:n],
                                 wd_rows[:, :, q * FQ:q * FQ + n]).then_inc(wd_landed, 16)

            load_wd(0)
            load_wd(1)
            sp.wait_ge(td_loed, 2)
            for q in range(4):
                sp.dma_start(wq_int[q * Q:(q + 1) * Q, :, :],
                             wq.rearrange("(b r) (q c) -> q r b c", r=Q, q=4)[q]).then_inc(wq_landed, 16)
            sp.wait_ge(stack_loed, FT)
            sp.dma_start(bias_t[:, :], bias.rearrange("(a n) -> a n", a=1).broadcast_to([P, H])).then_inc(bias_landed, 16)

            def load_res(n):
                if n >= 4:
                    sp.wait_ge(out_stored[n % 4], 16 * (n // 4))
                sp.dma_start(res[:, n % 4, :], x_flat[n * P:(n + 1) * P, :]).then_inc(res_landed[n % 4], 16)

            for n in range(4):
                load_res(n)
            load_wd(2)
            load_wd(3)
            for n in range(NB):
                sp.wait_ge(y_added, n + 1)
                sp.dma_start(out_flat[n * P:(n + 1) * P, :], res[:, n % 4, :]).then_inc(out_stored[n % 4], 16)
                if n + 4 < NB:
                    load_res(n + 4)
            for s in range(4):
                sp.wait_ge(out_stored[s], 16 * (NB // 4))

        @block.gpsimd
        def _(pool):
            pool.dma_start(idx_all[:, :], idx_row.broadcast_to([P, NB])).then_inc(idx_landed, 16)
            nc.gpsimd.memset(ident[:, :], 0.0).then_inc(consts, 1)
            nc.gpsimd.memset(own[:, :], 1.0).then_inc(consts, 1)
            nc.gpsimd.memset(mask[0:Q, :], LORA_SCALE).then_inc(consts, 1)
            pool.wait_ge(consts, 3)
            nc.gpsimd.affine_select(out=ident[:, :], in_=ident[:, :], compare_op=ALU.not_equal, fill=1.0, base=0,
                                    pattern=[[-1, P]], channel_multiplier=1).then_inc(ident_made, 1)
            nc.gpsimd.affine_select(out=own[:, :], in_=own[:, :], compare_op=ALU.is_ge, fill=0.0, base=0,
                                    pattern=[[-R, NB]], channel_multiplier=1).then_inc(consts, 1)
            pool.wait_ge(consts, 4)
            nc.gpsimd.affine_select(out=own[:, :], in_=own[:, :], compare_op=ALU.is_ge, fill=0.0, base=R - 1,
                                    pattern=[[R, NB]], channel_multiplier=-1).then_inc(consts, 1)
            nc.gpsimd.iota(row_off[:, :], pattern=[[-R, NB]], base=0, channel_multiplier=1,
                           allow_small_or_imprecise_dtypes=True).then_inc(consts, 1)
            nc.gpsimd.affine_select(out=mask[0:Q, 0:T], in_=mask[0:Q, 0:T], compare_op=ALU.is_ge, fill=0.0,
                                    base=R - 1, pattern=[[0, T]], channel_multiplier=-1).then_inc(consts, 1)
            nc.gpsimd.affine_select(out=mask[0:Q, T:PT], in_=mask[0:Q, T:PT], compare_op=ALU.is_ge, fill=0.0,
                                    base=-R, pattern=[[0, T]], channel_multiplier=1).then_inc(consts, 1)
            ids = load_ids(pool)
            pool.wait_ge(rows_made, 4)
            for table, dst, landed in ((a_gate, a_in[:, 0, :], a_landed[0]), (a_up, a_in[:, 1, :], a_landed[1]),
                                       (a_down, ad_rows[:, :], ad_landed)):
                pool.indirect_dma_start(
                    out=dst, out_offset=None, in_=table.rearrange("l a r n -> (l a r) n"),
                    in_offset=bass.IndirectOffsetOnAxis(ap=row_id[:, 0:1], axis=0)).then_inc(landed, 16)
            load_b(pool, b_up_landed, 1, range(NB // 2), ids)
            load_w(pool, up_landed, 1, 1, 1)

            def period(tile):
                j, use, slot = tile
                pool.wait_ge(w_tred, j * 2)
                load_w(pool, up_landed, 1, j + 2, slot)

            for j in range(1, PROLOGUE_TILES):
                period(peeled(j))
            for b in range(NB):
                pool.dma_start(bd_in[3 * Q:P, b // 2, b % 2, :, :],
                               b_down[0, ids[b]].rearrange("(q r t) c -> r q (t c)", q=4, r=Q)).then_inc(bd_landed, 16)
            with pool.Fori(0, ROUNDS - 1) as i:
                for step in range(2):
                    period(in_loop(i, step))
            period(peeled(FT - 4))
            pool.wait_ge(w_tred, 2 * (FT - 3))
            load_w(pool, up_landed, 1, FT - 1, (FT - 1) % 2, last=True)
            for q in range(4):
                for src, dst in ((scale, scale_t), (zero_point, zero_t)):
                    pool.dma_start(dst[q * Q:(q + 1) * Q, :], src.rearrange("(b r) g -> g r b", r=Q)[q],
                                   allow_slow_non_contiguous=True).then_inc(sz_landed, 16)
            pool.wait_ge(bias_landed, 16)
            for n in range(NB):
                pool.wait_ge(res_landed[n % 4], 16 * (n // 4 + 1))
                nc.gpsimd.tensor_tensor(res[:, n % 4, :], res[:, n % 4, :], bias_t[:, :], ALU.add).then_inc(biased, 1)

        @block.scalar
        def _(act):
            def x_part(h):
                for k in range(KT):
                    act.wait_ge(x_tred, KT * h + k + 1)
                    nc.scalar.copy(xt_hi[:, k, h * HALF:(h + 1) * HALF], x_ps[h][k][:, :]).then_inc(x_hied, 1)

            def w_part(tile, quads=4):
                j, use, slot = tile
                for g in range(2):
                    act.wait_ge(w_tred, j * 2 + (g - 1))
                    nc.scalar.copy(w_hi[:, slot, g, :, 0:quads * Q], w_tr[:, g, :, 0:quads * Q]).then_inc(w_hied, 1)

            def b_part(tile, quads=4):
                j, use, slot = tile
                m = quads * Q
                src = b_tr[:, :, 0:quads * FQ].rearrange("p g (q j r) -> p g q j r", q=quads, j=FT)[:, :, :, j, :]

                def by_quad(ap):
                    return ap.rearrange("p g (q r) -> p g q r", q=quads)

                nc.scalar.copy(by_quad(b_hi[:, :, 0:m]), src).then_inc(b_hied, 1)
                for p in range(PAIRS):
                    for s in range(2):
                        last = nc.scalar.copy(by_quad(b_stack[s * Q:(s + 1) * Q, slot, p, :, 0:m]),
                                              src[p * Q:(p + 1) * Q])
                last.then_inc(stack_hied, 1)

            def t_part(h):
                act.wait_ge(bank_read, h + 1)
                nc.scalar.copy(t_hi[:, h, :], t_val[:, h, :]).then_inc(t_hied, 1)
                for p in range(2):
                    for g in range(2):
                        for s in (0, 2):
                            last = nc.scalar.copy(
                                t_stack[s * Q:(s + 1) * Q, g, h * HALF + p * PT:h * HALF + (p + 1) * PT],
                                t_val[(2 * p + g) * Q:(2 * p + g + 1) * Q, h, :])
                last.then_inc(ts_hied, 1)

            def ad_part(j, slot, rows=P):
                last = nc.scalar.copy(ad_parts[0:rows, slot, :, :, 0, :],
                                      ad_tr[0:rows, :, j, :].rearrange("p (h a) r -> p h a r", h=2))
                last.then_inc(ad_hied, 1)

            def ad_last():
                act.wait_ge(unit_done, 2 * (FT - 1))
                nc.scalar.copy(ad_tail[0:KL, :, :, 0, :],
                               ad_tr[0:KL, :, FT - 1, :].rearrange("p (h a) r -> p h a r", h=2)).then_inc(ad_hied, 1)

            def evacuate(j):
                for h in range(2):
                    act.wait_ge(unit_done, j * 2 + (h + 1))
                    nc.scalar.activation(silu[:, h, :], gate_ps[h][:, :], ACT.Silu).then_inc(silu_done, 1)
                    act.wait_ge(act_done, j * 2 + (h + 1))
                    nc.scalar.copy(act_hi[:, j, h * HALF:(h + 1) * HALF], actf[:, h, :]).then_inc(act_hied, 1)

            def evacuate_last():
                j = FT - 1
                for h in range(2):
                    act.wait_ge(unit_done, 2 * j + h + 1)
                    nc.scalar.activation(silu[0:KL, h, :], gate_ps[h][0:KL, :], ACT.Silu).then_inc(silu_done, 1)
                    act.wait_ge(act_done, 2 * j + h + 1)
                    nc.scalar.copy(act_hi[0:KL, j, h * HALF:(h + 1) * HALF], actf[0:KL, h, :]).then_inc(act_hied, 1)

            act.wait_ge(scratch_set, 1)
            nc.scalar.activation(silu[0:1, 0, 0:1], silu[0:1, 0, 1:2], ACT.Silu)
            x_part(0)
            for g in range(2):
                act.wait_ge(first_tred, g + 1)
                nc.scalar.copy(w_hi[:, 0, g, :, :], w_ps[g][:, :].rearrange("p (k m) -> p k m", k=KT)
                               ).then_inc(w_hied, 1)
            x_part(1)
            for g in range(2):
                act.wait_ge(a_tred, g + 1)
                nc.scalar.copy(a_hi[:, :, :, g, :],
                               a_ps[g][:, :].rearrange("p (k a c) -> p k a c", k=KT, a=PAIRS)).then_inc(a_hied, 1)
            t_part(0)
            t_part(1)
            act.wait_ge(b_tred, 2)
            b_part(peeled(0))

            def period(tile, after, quads=4):
                j, use, slot = tile
                if not isinstance(j, int) or j >= 1:
                    act.wait_ge(unit_done, j * 2)
                w_part(after, quads)
                if isinstance(j, int) and j == 0:
                    evacuate(j)
                    b_part(after, quads)
                    return
                b_part(after, quads)
                if isinstance(j, int) and j == 1:
                    act.wait_ge(ad_tred, 1)
                if not isinstance(j, int) or j >= 3:
                    act.wait_ge(td_used, j - 2)
                ad_part(j - 1, 1 - slot)
                evacuate(j)

            for j in range(PROLOGUE_TILES):
                period(peeled(j), peeled(j + 1))
            with act.Fori(0, ROUNDS) as i:
                for step in range(2):
                    period(in_loop(i, step), in_loop(i, step + 1))
            period(peeled(FT - 2), peeled(FT - 1), 3)

            def wd_part(t):
                act.wait_ge(wd_tred, t + 1)
                s = t % 2
                nc.scalar.copy(wl_hi[s][3 * Q:P, :, :], bd_tr[3 * Q:P, :, t, :])
                nc.scalar.copy(wl_hi[s][0:KL, :, :],
                               wd_tr[0:KL, FT - 1:FT, :].broadcast_to([KL, PAIRS, P]))
                nc.scalar.copy(wd_hi[s][:, :, :], wd_tr[:, 0:FT - 1, :]).then_inc(wd_hied, 1)

            act.wait_ge(td_used, FT - 3)
            ad_part(FT - 2, (FT - 2) % 2)
            ad_last()
            wd_part(0)
            evacuate_last()
            for h in range(2):
                act.wait_ge(td_done, h + 1)
                for p in range(2):
                    cols = slice(p * PT, (p + 1) * PT)
                    nc.scalar.copy(td_a[h][3 * Q:P, cols], td_ps[h][2 * p * Q:(2 * p + 1) * Q, cols])
                    last = nc.scalar.copy(td_b[h][3 * Q:P, cols], td_ps[h][(2 * p + 1) * Q:(2 * p + 2) * Q, cols])
                last.then_inc(td_copied, 1)
                act.wait_ge(td_masked, h + 1)
                nc.scalar.copy(act_hi[3 * Q:P, FT - 1, h * HALF:(h + 1) * HALF], td_a[h][3 * Q:P, :]).then_inc(td_hied, 1)

            def down_part(t):
                for h in range(2):
                    act.wait_ge(down_done, 2 * t + h + 1)
                    nc.scalar.copy(dt_hi[:, t, h * HALF:(h + 1) * HALF], down_ps[h][:, :]).then_inc(down_hied, 1)

            for t in range(KT - 1):
                wd_part(t + 1)
                down_part(t)
            for t in range(KT):
                act.wait_ge(wq_tred, t + 1)
                nc.scalar.copy(wq_hi[:, t, :], wq_tr[:, t % 2, :]).then_inc(wq_hied, 1)
            down_part(KT - 1)

        @block.vector
        def _(dve):
            SUB = ALU.subtract

            def x_part(h):
                for k in range(KT):
                    dve.wait_ge(x_hied, KT * h + k + 1)
                    cols = slice(h * HALF, (h + 1) * HALF)
                    nc.vector.tensor_tensor(xt_lo[:, k, cols], x_ps[h][k][:, :], xt_hi[:, k, cols].bitcast(F32),
                                            SUB).then_inc(x_loed, 1)

            def w_transpose(tile, quads=4):
                j, use, slot = tile
                w_loads, up_loads = use + (1 - slot), use - (1 - slot)
                if quads == 4:
                    dve.wait_ge(w_landed[slot], w_loads * W_LOAD)
                    if not isinstance(j, int) or j != 2:
                        dve.wait_ge(up_landed[slot], up_loads * W_LOAD)
                else:
                    dve.wait_ge(w_landed[slot], (w_loads - 1) * W_LOAD + W_LAST)
                    dve.wait_ge(up_landed[slot], (up_loads - 1) * W_LOAD + W_LAST)
                for g in range(2):
                    nc.vector.transpose(
                        w_tr[:, g, :, 0:quads * Q].rearrange("p k (a r) -> p a k r", r=Q),
                        w_in[:, slot, g, 0:quads, :].rearrange("p a (r k) -> p a k r", k=KT)).then_inc(w_tred, 1)

            def w_part(tile, quads=4):
                j, use, slot = tile
                for g in range(2):
                    dve.wait_ge(w_hied, j * 2 + (g + 1))
                    m = quads * Q
                    nc.vector.tensor_tensor(w_lo[:, slot, g, :, 0:m], w_tr[:, g, :, 0:m],
                                            w_hi[:, slot, g, :, 0:m].bitcast(F32), SUB).then_inc(w_loed, 1)

            def b_part(tile, quads=4):
                j, use, slot = tile
                dve.wait_ge(b_hied, j + 1)
                m = quads * Q
                src = b_tr[:, :, 0:quads * FQ].rearrange("p g (q j r) -> p g q j r", q=quads, j=FT)[:, :, :, j, :]

                def by_quad(ap):
                    return ap.rearrange("p g (q r) -> p g q r", q=quads)

                nc.vector.tensor_tensor(by_quad(b_lo[:, :, 0:m]), src, by_quad(b_hi[:, :, 0:m]).bitcast(F32),
                                        SUB).then_inc(b_loed, 1)
                dve.wait_ge(b_loed, j + 1)
                for p in range(PAIRS):
                    last = nc.vector.tensor_copy(b_stack[2 * Q:3 * Q, slot, p, :, 0:m],
                                                 b_lo[p * Q:(p + 1) * Q, :, 0:m].bitcast(F32))
                last.then_inc(stack_loed, 1)

            def ad_part(j, slot, rows=P):
                dve.wait_ge(ad_hied, j + 1)
                nc.vector.tensor_tensor(ad_parts[0:rows, slot, :, :, 1, :],
                                        ad_tr[0:rows, :, j, :].rearrange("p (h a) r -> p h a r", h=2),
                                        ad_parts[0:rows, slot, :, :, 0, :].bitcast(F32), SUB).then_inc(ad_loed, 1)

            def evacuate(j, rows=P):
                for h in range(2):
                    dve.wait_ge(silu_done, j * 2 + (h + 1))
                    nc.vector.tensor_tensor(actf[0:rows, h, :], up_ps[h][0:rows, :], silu[0:rows, h, :],
                                            ALU.mult).then_inc(act_done, 1)
                    dve.wait_ge(act_hied, j * 2 + (h + 1))
                    cols = slice(h * HALF, (h + 1) * HALF)
                    nc.vector.tensor_tensor(act_lo[0:rows, j, cols], actf[0:rows, h, :],
                                            act_hi[0:rows, j, cols].bitcast(F32), SUB).then_inc(act_loed, 1)

            def t_mask(h):
                dve.wait_ge(t_done, h + 1)
                for p in range(2):
                    rows = slice(2 * p * Q, 2 * (p + 1) * Q)
                    last = nc.vector.tensor_tensor(t_val[rows, h, :], t_ps[h][rows, p * PT:(p + 1) * PT],
                                                   mask[rows, :], ALU.mult)
                last.then_inc(bank_read, 1)

            def t_part(h):
                dve.wait_ge(t_hied, h + 1)
                nc.vector.tensor_tensor(t_lo[:, h, :], t_val[:, h, :], t_hi[:, h, :].bitcast(F32),
                                        SUB).then_inc(t_loed, 1)
                dve.wait_ge(t_loed, h + 1)
                for p in range(2):
                    for g in range(2):
                        last = nc.vector.tensor_copy(
                            t_stack[Q:2 * Q, g, h * HALF + p * PT:h * HALF + (p + 1) * PT],
                            t_lo[(2 * p + g) * Q:(2 * p + g + 1) * Q, h, :].bitcast(F32))
                last.then_inc(ts_loed, 1)

            nc.vector.memset(silu[0:1, 0, 0:2], 0.0).then_inc(scratch_set, 1)
            dve.wait_ge(consts, 8)
            dve.wait_ge(idx_landed, 16)
            nc.vector.scalar_tensor_tensor(out=row_all[:, :], in0=idx_all[:, :], scalar=float(R), in1=row_off[:, :],
                                           op0=ALU.mult, op1=ALU.add).then_inc(rows_made, 1)
            dve.wait_ge(rows_made, 1)
            nc.vector.tensor_tensor(row_own[:, :], row_all[:, :], own[:, :], ALU.mult).then_inc(rows_made, 1)
            dve.wait_ge(rows_made, 2)
            nc.vector.reduce_sum(row_sum[:, 0:1], row_own[:, :], axis=mybir.AxisListType.X).then_inc(rows_made, 1)
            dve.wait_ge(rows_made, 3)
            nc.vector.tensor_copy(row_id[:, 0:1], row_sum[:, 0:1]).then_inc(rows_made, 1)
            for q in range(1, 4):
                last = nc.vector.tensor_copy(mask[q * Q:(q + 1) * Q, :], mask[0:Q, :])
            last.then_inc(mask_made, 1)
            x_part(0)
            for g in range(2):
                dve.wait_ge(w_hied, g + 1)
                nc.vector.tensor_tensor(w_lo[:, 0, g, :, :], w_ps[g][:, :].rearrange("p (k m) -> p k m", k=KT),
                                        w_hi[:, 0, g, :, :].bitcast(F32), SUB).then_inc(w_loed, 1)
            x_part(1)
            for g in range(2):
                dve.wait_ge(a_hied, g + 1)
                nc.vector.tensor_tensor(a_lo[:, :, :, g, :],
                                        a_ps[g][:, :].rearrange("p (k a c) -> p k a c", k=KT, a=PAIRS),
                                        a_hi[:, :, :, g, :].bitcast(F32), SUB).then_inc(a_loed, 1)
            dve.wait_ge(ad_landed, 16)
            for q in range(4):
                n = FQ if q < 3 else LAST
                for p in range(PAIRS):
                    last = nc.vector.tensor_copy(ad_in[q * Q:(q + 1) * Q, p, 0:n],
                                                 ad_rows[p * Q:(p + 1) * Q, q * FQ:q * FQ + n])
            last.then_inc(ad_moved, 1)
            dve.wait_ge(mask_made, 1)
            for h in range(2):
                t_mask(h)
                t_part(h)
            for g in range(2):
                if g == 0:
                    dve.wait_ge(b_landed, (NB + NB // 2) * B_LOAD)
                    dve.wait_ge(b_up_landed, NB // 2 * B_LOAD)
                nc.vector.transpose(b_tr[:, g, 0:F].rearrange("p (b r) -> p b r", r=Q),
                                    b_in[:, g, :, :].rearrange("p e (b c) -> p b e c", c=R)).then_inc(b_tred, 1)
            b_part(peeled(0))

            def period(tile, after, quads=4):
                j, use, slot = tile
                w_transpose(after, quads)
                w_part(after, quads)
                if isinstance(j, int) and j == 0:
                    evacuate(j)
                    b_part(after, quads)
                    return
                b_part(after, quads)
                if isinstance(j, int) and j == 1:
                    dve.wait_ge(ad_moved, 1)
                    for a in range(PAIRS):
                        nc.vector.transpose(ad_tr[0:KL, a, :, :], ad_in[0:KL, a, :].rearrange("p (r j) -> p j r", j=FT))
                        last = nc.vector.transpose(ad_tr[KL:P, a, 0:NL, :],
                                                   ad_in[KL:P, a, 0:LAST].rearrange("p (r j) -> p j r", j=NL))
                    last.then_inc(ad_tred, 1)
                ad_part(j - 1, 1 - slot)
                evacuate(j)

            for j in range(PROLOGUE_TILES):
                period(peeled(j), peeled(j + 1))
            dve.wait_ge(bd_landed, NB * 16)
            for a in range(PAIRS):
                for t in range(KT):
                    last = nc.vector.transpose(
                        bd_tr[KL:P, a, t, :].rearrange("p (q r) -> p q r", q=4),
                        bd_in[KL:P, a, :, :, t * R:(t + 1) * R].rearrange("p e q c -> p q e c"))
            last.then_inc(bd_tred, 1)
            with dve.Fori(0, ROUNDS) as i:
                for step in range(2):
                    period(in_loop(i, step), in_loop(i, step + 1))
            period(peeled(FT - 2), peeled(FT - 1), 3)

            def wd_transpose(t):
                dve.wait_ge(wd_landed, (t + 1) * 4 * 16)
                if t:
                    dve.wait_ge(wd_loed, t)
                if t == 1:
                    dve.wait_ge(unit_done, 2 * FT)
                if t >= 2:
                    dve.wait_ge(down_done, 2 * (t - 1))
                for q in range(4):
                    cols = slice(q * Q, (q + 1) * Q)
                    nc.vector.transpose(wd_tr[0:KL, :, cols], wd_in[0:KL, q, :].rearrange("p (r j) -> p j r", j=FT))
                    last = nc.vector.transpose(wd_tr[KL:P, 0:NL, cols],
                                               wd_in[KL:P, q, 0:LAST].rearrange("p (r j) -> p j r", j=NL))
                last.then_inc(wd_tred, 1)

            def wd_part(t):
                s = t % 2
                dve.wait_ge(wd_hied, t + 1)
                nc.vector.tensor_tensor(wl_lo[s][KL:P, :, :], bd_tr[KL:P, :, t, :],
                                        wl_hi[s][KL:P, :, :].bitcast(F32), SUB)
                nc.vector.tensor_tensor(wl_lo[s][0:KL, :, :], wd_tr[0:KL, FT - 1:FT, :].broadcast_to([KL, PAIRS, P]),
                                        wl_hi[s][0:KL, :, :].bitcast(F32), SUB)
                nc.vector.tensor_tensor(wd_lo[s][:, :, :], wd_tr[:, 0:FT - 1, :], wd_hi[s][:, :, :].bitcast(F32),
                                        SUB).then_inc(wd_loed, 1)

            ad_part(FT - 2, (FT - 2) % 2)
            dve.wait_ge(ad_hied, FT)
            nc.vector.tensor_tensor(ad_tail[0:KL, :, :, 1, :],
                                    ad_tr[0:KL, :, FT - 1, :].rearrange("p (h a) r -> p h a r", h=2),
                                    ad_tail[0:KL, :, :, 0, :].bitcast(F32), SUB).then_inc(ad_loed, 1)
            wd_transpose(0)
            wd_part(0)
            evacuate(FT - 1, KL)
            def td_part(h):
                dve.wait_ge(td_copied, h + 1)
                nc.vector.tensor_tensor(td_a[h][KL:P, :], td_a[h][KL:P, :], td_b[h][KL:P, :], ALU.add).then_inc(td_summed, 1)
                dve.wait_ge(td_summed, h + 1)
                for p in range(2):
                    cols = slice(p * PT, (p + 1) * PT)
                    last = nc.vector.tensor_tensor(td_a[h][KL:P, cols], td_a[h][KL:P, cols], mask[KL:P, :], ALU.mult)
                last.then_inc(td_masked, 1)
                dve.wait_ge(td_hied, h + 1)
                cols = slice(h * HALF, (h + 1) * HALF)
                nc.vector.tensor_tensor(act_lo[KL:P, FT - 1, cols], td_a[h][KL:P, :],
                                        act_hi[KL:P, FT - 1, cols].bitcast(F32), SUB).then_inc(td_loed, 1)

            def down_part(t):
                for h in range(2):
                    dve.wait_ge(down_hied, 2 * t + h + 1)
                    cols = slice(h * HALF, (h + 1) * HALF)
                    nc.vector.tensor_tensor(dt_lo[:, t, cols], down_ps[h][:, :], dt_hi[:, t, cols].bitcast(F32),
                                            SUB).then_inc(bank_read, 1)

            td_part(0)
            wd_transpose(1)
            td_part(1)
            wd_part(1)
            down_part(0)
            for t in range(1, KT - 1):
                wd_transpose(t + 1)
                wd_part(t + 1)
                down_part(t)
            dve.wait_ge(wq_landed, 4 * 16)
            dve.wait_ge(sz_landed, 2 * 4 * 16)
            nc.vector.tensor_tensor(wq_val[:, :, :], wq_int[:, :, :],
                                    zero_t[:, :].unsqueeze(2).broadcast_to([P, 16, P]), SUB).then_inc(wq_zeroed, 1)
            dve.wait_ge(wq_zeroed, 1)
            nc.vector.tensor_tensor(wq_val[:, :, :], wq_val[:, :, :],
                                    scale_t[:, :].unsqueeze(2).broadcast_to([P, 16, P]), ALU.mult).then_inc(wq_scaled, 1)
            dve.wait_ge(wq_scaled, 1)
            for t in range(KT):
                nc.vector.transpose(wq_tr[:, t % 2, :].rearrange("p (b r) -> p b r", r=Q),
                                    wq_val[:, :, :].rearrange("p b (r t) -> p b r t", t=KT)[:, :, :, t]).then_inc(wq_tred, 1)
                dve.wait_ge(wq_hied, t + 1)
                nc.vector.tensor_tensor(wq_lo[:, t, :], wq_tr[:, t % 2, :], wq_hi[:, t, :].bitcast(F32),
                                        SUB).then_inc(wq_loed, 1)
            down_part(KT - 1)
            for n in range(NB):
                dve.wait_ge(y_done, n + 1)
                dve.wait_ge(biased, n + 1)
                nc.vector.tensor_tensor(res[:, n % 4, :], y_ps[n % 4][:, :], res[:, n % 4, :], ALU.add).then_inc(y_added, 1)

        @block.tensor
        def _(pe):
            mm = nc.tensor.matmul

            def project_t(h):
                pe.wait_ge(x_loed, KT * (h + 1))
                pe.wait_ge(a_loed, 2)
                cols = slice(h * HALF, (h + 1) * HALF)
                n = 0
                for w, v in ((a_hi, xt_hi), (a_hi, xt_lo), (a_lo, xt_hi)):
                    for k in range(KT):
                        last = mm(t_ps[h][:, :], w[:, k, 2 * h:2 * h + 2, :, :], v[:, k, cols],
                                  start=n == 0, stop=n == 3 * KT - 1)
                        n += 1
                last.then_inc(t_done, 1)

            products = [(w, v, k) for w, v in ((w_hi, xt_hi), (w_hi, xt_lo), (w_lo, xt_hi)) for k in range(KT)]

            def weights(tile, h, m=P, gates=(0, 1)):
                j, use, slot = tile
                first = isinstance(j, int) and j == 0
                if first:
                    pe.wait_ge(x_loed, KT * (h + 1))
                else:
                    pe.wait_ge(act_done, j * 2 + (h - 1))
                for g in gates:
                    ps = (gate_ps[h], up_ps[h])[g]
                    pe.wait_ge(w_hied, j * 2 + (g + 1))
                    for n, (w, v, k) in enumerate(products[:-1]):
                        if n == 2 * KT:
                            pe.wait_ge(w_loed, j * 2 + (g + 1))
                        mm(ps[0:m, :], w[:, slot, g, k, 0:m], v[:, k, h * HALF:(h + 1) * HALF],
                           start=n == 0, stop=False)

            def adapters(tile, h, m=P):
                j, use, slot = tile
                pe.wait_ge(stack_hied, j + 1)
                pe.wait_ge(stack_loed, j + 1)
                pe.wait_ge(ts_hied, h + 1)
                pe.wait_ge(ts_loed, h + 1)
                w, v, k = products[-1]
                for g, ps in enumerate((gate_ps[h], up_ps[h])):
                    for p in range(2):
                        toks = slice(h * HALF + p * PT, h * HALF + (p + 1) * PT)
                        mm(ps[0:m, p * PT:(p + 1) * PT], b_stack[0:KL, slot, 2 * h + p, g, 0:m],
                           t_stack[0:KL, g, toks], start=False, stop=False, skip_group_check=True)
                    last = mm(ps[0:m, :], w[:, slot, g, k, 0:m], v[:, k, h * HALF:(h + 1) * HALF],
                              start=False, stop=True)
                last.then_inc(unit_done, 1)

            def project_act(j, w, h, rows=P, first=False, last_tile=False):
                pe.wait_ge(act_loed, j * 2 + (h + 1))
                pe.wait_ge(ad_loed, j + 1)
                cols = slice(h * HALF, (h + 1) * HALF)
                w = w[0:rows, h, :, :, :]
                mm(td_ps[h][:, :], w, act_hi[0:rows, j, cols], start=first, stop=False, skip_group_check=True)
                last = mm(td_ps[h][:, :], w, act_lo[0:rows, j, cols], start=False, stop=last_tile,
                          skip_group_check=True)
                if last_tile:
                    last.then_inc(td_done, 1)
                elif h == 1:
                    last.then_inc(td_used, 1)

            def transpose(ps, c, rows):
                return nc.tensor.transpose(ps[:, c * P:(c + 1) * P], rows, ident[:, :])

            def tile_of(ap, k):
                return ap.rearrange("p (m k) -> p k m", k=KT)[:, k]

            def transpose_x(h):
                for k in range(KT):
                    for b in range(NB // 2):
                        if k == 0 and b % 2 == 0:
                            pe.wait_ge(x_landed[2 * h + b // 2], 16)
                        last = transpose(x_ps[h][k], b, tile_of(x_in[:, h * NB // 2 + b, :], k))
                    last.then_inc(x_tred, 1)

            pe.wait_ge(ident_made, 1)
            transpose_x(0)
            for g in range(2):
                pe.wait_ge(first_landed[g], 2 * 16)
                for k in range(KT):
                    last = transpose(w_ps[g], k, tile_of(w_first[:, g, :], k))
                last.then_inc(first_tred, 1)
            weights(peeled(0), 0, gates=(0,))
            pe.wait_ge(w_loed, 2)
            transpose_x(1)
            weights(peeled(0), 0, gates=(1,))
            for g in range(2):
                pe.wait_ge(a_landed[g], 16)
                for k in range(KT):
                    last = transpose(a_ps[g], k, tile_of(a_in[:, g, :], k))
                last.then_inc(a_tred, 1)
            weights(peeled(0), 1, gates=(0,))
            for h in range(2):
                project_t(h)
            weights(peeled(0), 1, gates=(1,))
            for h in range(2):
                adapters(peeled(0), h)

            for h in range(2):
                weights(peeled(1), h)
                adapters(peeled(1), h)
            for h in range(2):
                weights(peeled(2), h)
                adapters(peeled(2), h)
                project_act(0, ad_parts[:, 0], h, first=True)
            with pe.Fori(0, ROUNDS) as i:
                for step in range(2):
                    tile = in_loop(i, step)
                    for h in range(2):
                        weights(tile, h)
                        adapters(tile, h)
                        project_act(i * 2 + (PROLOGUE_TILES + step - 2), ad_parts[:, tile[2]], h)
            for h in range(2):
                weights(peeled(FT - 2), h)
                adapters(peeled(FT - 2), h)
                project_act(FT - 4, ad_parts[:, FT % 2], h)
            for h in range(2):
                weights(peeled(FT - 1), h, KL)
                adapters(peeled(FT - 1), h, KL)
            for j in (FT - 3, FT - 2):
                for h in range(2):
                    project_act(j, ad_parts[:, j % 2], h)
            for h in range(2):
                project_act(FT - 1, ad_tail, h, rows=KL, last_tile=True)

            with pe.Fori(0, KT // 2) as i:
                for s in range(2):
                    for h in range(2):
                        group = i * 4 + (2 * s + h)
                        cols = slice(h * HALF, (h + 1) * HALF)
                        pe.wait_ge(wd_loed, i * 2 + (s + 1))
                        pe.wait_ge(bank_read, group + 1)
                        products = [(w, v, j) for w, v in ((wd_hi, act_hi), (wd_hi, act_lo), (wd_lo, act_hi))
                                    for j in range(FT - 1)]
                        for n, (w, v, j) in enumerate(products[:-1]):
                            mm(down_ps[h][:, :], w[s][:, j, :], v[:, j, cols], start=n == 0, stop=False)
                        pe.wait_ge(td_loed, h + 1)
                        for p in range(2):
                            toks = slice(h * HALF + p * PT, h * HALF + (p + 1) * PT)
                            for w, v in ((wl_hi, act_hi), (wl_hi, act_lo), (wl_lo, act_hi)):
                                mm(down_ps[h][:, p * PT:(p + 1) * PT], w[s][:, 2 * h + p, :],
                                   v[:, FT - 1, toks], start=False, stop=False, skip_group_check=True)
                        w, v, j = products[-1]
                        last = mm(down_ps[h][:, :], w[s][:, j, :], v[:, j, cols], start=False, stop=True)
                        last.then_inc(down_done, 1)

            pe.wait_ge(wq_loed, KT)
            for n in range(NB):
                pe.wait_ge(bank_read, 2 + 2 * KT - 1 + n // (NB // 2))
                if n >= 4:
                    pe.wait_ge(y_added, n - 3)
                toks = slice(n * P, (n + 1) * P)
                c = 0
                for v, w in ((dt_hi, wq_hi), (dt_hi, wq_lo), (dt_lo, wq_hi)):
                    for t in range(KT):
                        last = mm(y_ps[n % 4][:, :], v[:, t, toks], w[:, t, :], start=c == 0, stop=c == 3 * KT - 1)
                        c += 1
                last.then_inc(y_done, 1)


_INS = ['x', 'itok_B_2_6', 'L0_cond_W_gate', 'L0_cond_W_up', 'L0_cond_W_down', 'L0_cond_A_gate', 'L0_cond_B_gate',
        'L0_cond_A_up', 'L0_cond_B_up', 'L0_cond_A_down', 'L0_cond_B_down', 'L0_ffn_weight_q', 'L0_ffn_scale',
        'L0_ffn_zero_point', 'L0_ffn_bias']
_OUT = ((NB, T, H), 'float32')


def kernel(**inputs):
    import numpy as _np
    import concourse.bacc as _bacc
    from concourse import mybir as _mybir
    from concourse.bass_utils import run_bass_kernel_spmd as _run

    nc = _bacc.Bacc("TRN2", target_bir_lowering=False, num_devices=1)
    arrays, args = {}, []
    for name in _INS:
        a = _np.ascontiguousarray(inputs[name])
        arrays[f"in_{name}"] = a
        args.append(nc.dram_tensor(f"in_{name}", a.shape, _mybir.dt.from_np(a.dtype), kind="ExternalInput").ap())
    out = nc.dram_tensor("out_y", _OUT[0], _mybir.dt.from_np(_np.dtype(_OUT[1])), kind="ExternalOutput").ap()
    adaln_ffn(nc, *args, out)
    r = _run(nc, [arrays], core_ids=[0])
    return r.results[0]["out_y"]
```

```python
from contextlib import ExitStack

import concourse.bass as bass
from concourse import mybir

F32 = mybir.dt.float32
F32R = mybir.dt.float32r
I32 = mybir.dt.int32
ALU = mybir.AluOpType
ACT = mybir.ActivationFunctionType

P = 128
Q = 32
NB, T, H, F, R = 8, 128, 512, 1376, 16
ADAPTERS = 16
NT = NB * T
HALF = NT // 2
KT = H // P
FB = F // Q
FT = -(-FB // 4)
FQ = FT * Q
F3 = 3 * FQ
LAST = F - F3
NL = LAST // Q
KL = 3 * Q
PAIRS = NB // 2
PT = 2 * T
LORA_SCALE = 0.5
POOLS_B = 5
WARM_UPS = 6
PROLOGUE_TILES = 3


def adaln_ffn(nc, x, idx, w_gate, w_up, w_down, a_gate, b_gate, a_up, b_up, a_down, b_down,
              wq, scale, zero_point, bias, out):
    gu_w = (w_gate, w_up)
    gu_b = (b_gate, b_up)
    x_flat = x.rearrange("b t h -> (b t) h")
    out_flat = out.rearrange("b t h -> (b t) h")
    idx_row = idx.rearrange("(a b) -> a b", a=1)

    with ExitStack() as ctx:
        size = 212736
        arena = ctx.enter_context(nc.sbuf_tensor("arena", [P, size // 4], F32))
        base = nc.sbuf_base - size
        base = (base + 31) // 32 * 32
        places = {}
        top = [0]

        def room(name, nbytes):
            places[name] = base + top[0]
            top[0] += nbytes
            assert top[0] <= size, (name, top[0])

        def at(name, place, shape, dt=F32, plus=0):
            return nc.alloc_sbuf_tensor_at(name, shape, dt, offset=places[place] + plus)

        room("tokens", 2 * KT * NT * 4)
        room("act", 2 * FT * NT * 4)
        room("wring", 2 * 2 * 2 * KT * P * 4)
        room("wx", 2 * 2 * KT * P * 4)
        room("wy", 2 * KT * P * 4)
        room("temps", 4 * HALF * 4)
        room("by", 2 * FQ * 4 * 4)
        room("bhl", 2 * 2 * P * 4)
        room("sring", 2 * PAIRS * 2 * P * 4)
        room("ady", PAIRS * FQ * 4)
        room("adring", 2 * 2 * P * 4)
        room("tstack", 2 * NT * 4)
        room("wd0", 2 * (FT - 1) * P * 4 + PAIRS * 2 * P * 4)
        room("mask", PT * 4)
        room("sz", 2 * 4 * KT * 4)

        xt_hi = at("xt_hi", "tokens", [P, KT, NT], F32R)
        xt_lo = at("xt_lo", "tokens", [P, KT, NT], F32R, KT * NT * 4)
        dt_hi = at("dt_hi", "tokens", [P, KT, NT], F32R)
        dt_lo = at("dt_lo", "tokens", [P, KT, NT], F32R, KT * NT * 4)
        act_hi = at("act_hi", "act", [P, FT, NT], F32R)
        act_lo = at("act_lo", "act", [P, FT, NT], F32R, FT * NT * 4)
        early = 2 * NT * 4
        x_in = at("x_in", "act", [P, NB // 2, H], F32, early)
        x_quad = at("x_quad", "act", [P, HALF // Q, P], F32, early + 8192)
        x_tr = at("x_tr", "act", [P, KT, HALF])
        a_in = at("a_in", "act", [P, 2, H], F32, early + 16384)
        w_first = at("w_first", "act", [P, 2, H], F32, early + 20480)
        ad_rows = at("ad_rows", "act", [P, F], F32, early + 24576)
        ident = at("ident", "act", [P, P], F32, early + 30208)
        idx_all = at("idx_all", "act", [P, NB], I32, early + 30720)
        row_off = at("row_off", "act", [P, NB], F32, early + 30752)
        own = at("own", "act", [P, NB], F32, early + 30784)
        row_all = at("row_all", "act", [P, NB], F32, early + 30816)
        row_own = at("row_own", "act", [P, NB], F32, early + 30848)
        row_sum = at("row_sum", "act", [P, 1], F32, early + 30912)
        row_id = at("row_id", "act", [P, 1], mybir.dt.uint32, early + 30880)
        low = FT * NT * 4 + 3 * NT * 4
        b_in = at("b_in", "act", [P, 2, 2, FB * R], F32, low)
        a_hi = at("a_hi", "act", [P, KT, PAIRS, 2, Q], F32R, low + 11264)
        a_lo = at("a_lo", "act", [P, KT, PAIRS, 2, Q], F32R, low + 11264 + 4096)
        ad_in = at("ad_in", "act", [P, PAIRS, FQ], F32, low + 11264 + 8192)
        w_in = at("w_in", "wx", [P, 2, 2, 4, P])
        w_tr = at("w_tr", "wy", [P, 2, KT, P])
        w_hi = at("w_hi", "wring", [P, 2, 2, KT, P], F32R)
        w_lo = at("w_lo", "wring", [P, 2, 2, KT, P], F32R, 2 * 2 * KT * P * 4)
        silu = at("silu", "temps", [P, 2, HALF])
        actf = at("actf", "temps", [P, 2, HALF], F32, 2 * HALF * 4)
        b_tr = at("b_tr", "by", [P, 2, 4 * FQ])
        b_hi = at("b_hi", "bhl", [P, 2, P], F32R)
        b_lo = at("b_lo", "bhl", [P, 2, P], F32R, 2 * P * 4)
        b_stack = at("b_stack", "sring", [P, 2, PAIRS, 2, P], F32R)
        ad_tr = at("ad_tr", "ady", [P, PAIRS, FT, Q])
        ad_parts = at("ad_parts", "adring", [P, 2, 2, 2, 2, Q], F32R)
        ad_tail = at("ad_tail", "sring", [P, 2, 2, 2, Q], F32R, PAIRS * 2 * P * 4)
        t_stack = at("t_stack", "tstack", [P, 2, NT], F32R)
        bd_tr = at("bd_tr", "tstack", [P, PAIRS, KT, P])
        bd_in = at("bd_in", "wd0", [P, PAIRS, 2, 4, KT * R])
        t_val = at("t_val", "wd0", [P, 2, PT], F32, 8192)
        t_hi = at("t_hi", "wd0", [P, 2, PT], F32R, 8192 + 2048)
        t_lo = at("t_lo", "wd0", [P, 2, PT], F32R, 8192 + 4096)
        mask = at("mask_t", "mask", [P, PT])
        wd_in = at("wd_in", "by", [P, 4, FQ])
        wd_tr = at("wd_tr", "by", [P, FT, P], F32, 4 * FQ * 4)
        part = (FT - 1) * P * 4
        wd_hi = [at(f"wd_hi{s}", p, [P, FT - 1, P], F32R) for s, p in enumerate(("wd0", "wring"))]
        wd_lo = [at(f"wd_lo{s}", p, [P, FT - 1, P], F32R, part) for s, p in enumerate(("wd0", "wring"))]
        wl_hi = [at(f"wl_hi{s}", p, [P, PAIRS, P], F32R, 2 * part) for s, p in enumerate(("wd0", "wring"))]
        wl_lo = [at(f"wl_lo{s}", p, [P, PAIRS, P], F32R, 2 * part + PAIRS * P * 4)
                 for s, p in enumerate(("wd0", "wring"))]
        td_a = [at(f"td_a{h}", p, [P, HALF]) for h, p in enumerate(("wy", "temps"))]
        td_b = [at(f"td_b{h}", p, [P, HALF], F32, HALF * 4) for h, p in enumerate(("wy", "temps"))]
        wq_int = at("wq_int", "temps", [P, 16, P], I32)
        wq_val = at("wq_val", "temps", [P, 16, P], F32)
        wq_tr = at("wq_tr", "wy", [P, 2, H])
        wq_hi = at("wq_hi", "tstack", [P, KT, H], F32R)
        wq_lo = at("wq_lo", "sring", [P, KT, H], F32R)
        scale_t = at("scale_t", "sz", [P, 16])
        zero_t = at("zero_t", "sz", [P, 16], F32, 64)
        bias_t = at("bias_t", "bhl", [P, H])
        res = at("res", "wx", [P, 4, H])

        def bank(name):
            return ctx.enter_context(nc.psum_tensor(name, [P, HALF], F32))

        gate_ps = [bank(f"gate_ps{h}") for h in range(2)]
        up_ps = [bank(f"up_ps{h}") for h in range(2)]
        td_ps = [bank(f"td_ps{h}") for h in range(2)]
        down_ps = [bank(f"down_ps{h}") for h in range(2)]
        x_ps = [up_ps[0], up_ps[1], gate_ps[1], td_ps[0]]
        w_ps = [td_ps[1], down_ps[0]]
        a_ps = [down_ps[1], down_ps[0]]
        t_ps = down_ps
        y_ps = gate_ps + up_ps

        def sem(name):
            return ctx.enter_context(nc.semaphore(name))

        x_landed = [sem(f"x_landed{c}") for c in range(3)]
        x_half_landed = sem("x_half_landed")
        first_landed = [sem(f"first_landed{g}") for g in range(2)]
        w_landed = [sem(f"w_landed{s}") for s in range(2)]
        second_landed = sem("second_landed")
        up_landed = [sem(f"up_landed{s}") for s in range(2)]
        a_landed = [sem(f"a_landed{g}") for g in range(2)]
        b_landed = sem("b_landed")
        b_up_landed = sem("b_up_landed")
        ad_landed, bd_landed = (sem(n + "_landed") for n in ("ad", "bd"))
        idx_landed = sem("idx_landed")
        rows_made = sem("rows_made")
        wd_landed, wq_landed, sz_landed, bias_landed = (sem(n + "_landed") for n in ("wd", "wq", "sz", "bias"))
        res_landed = [sem(f"res_landed{s}") for s in range(4)]
        out_stored = [sem(f"out_stored{s}") for s in range(4)]
        consts = sem("consts")
        ident_made = sem("ident_made")
        mask_made = sem("mask_made")
        scratch_set = sem("scratch_set")

        x_tred, x_half_tred, x_hied, x_loed = sem("x_tred"), sem("x_half_tred"), sem("x_hied"), sem("x_loed")
        first_tred = sem("first_tred")
        stack_hied, stack_loed = sem("stack_hied"), sem("stack_loed")
        ts_hied, ts_loed = sem("ts_hied"), sem("ts_loed")
        a_tred, a_hied, a_loed = sem("a_tred"), sem("a_hied"), sem("a_loed")
        w_tred, w_hied, w_loed = sem("w_tred"), sem("w_hied"), sem("w_loed")
        b_tred, b_hied, b_loed = sem("b_tred"), sem("b_hied"), sem("b_loed")
        ad_moved = sem("ad_moved")
        ad_copied = sem("ad_copied")
        ad_tred, ad_hied, ad_loed = sem("ad_tred"), sem("ad_hied"), sem("ad_loed")
        t_done, t_hied, t_loed = sem("t_done"), sem("t_hied"), sem("t_loed")
        bank_read = sem("bank_read")
        gate_done = sem("gate_done")
        unit_done = sem("unit_done")
        silu_done, act_done, act_hied, act_loed = (sem(n) for n in ("silu_done", "act_done", "act_hied", "act_loed"))
        td_used = sem("td_used")
        td_done, td_copied, td_summed, td_masked, td_hied, td_loed = (
            sem(n) for n in ("td_done", "td_copied", "td_summed", "td_masked", "td_hied", "td_loed"))
        wd_tred, wd_hied, wd_loed = sem("wd_tred"), sem("wd_hied"), sem("wd_loed")
        down_done, down_hied = sem("down_done"), sem("down_hied")
        wq_zeroed, wq_scaled = sem("wq_zeroed"), sem("wq_scaled")
        wq_tred, wq_hied, wq_loed = sem("wq_tred"), sem("wq_hied"), sem("wq_loed")
        biased = sem("biased")
        y_done, y_added = sem("y_done"), sem("y_added")

        block = ctx.enter_context(nc.Block())

        W_LOAD = 4 * 2 * 16
        W_LAST = 4 * 16
        B_LOAD = 2 * 16

        def peeled(j):
            return j, (j + 1) // 2, j % 2

        def in_loop(i, step):
            first = PROLOGUE_TILES + step
            return i * 2 + first, i + (first + 1) // 2, first % 2

        ROUNDS = (FT - 2 - PROLOGUE_TILES) // 2

        def x_bank(xt, c):
            return xt[:, 2 * (c % 2):2 * (c % 2) + 2, c // 2 * PT:(c // 2 + 1) * PT]

        X_LOADS = ((0, 1), (1, 2), (2, 4))

        def load_x_half(eng):
            for q in range(4):
                eng.dma_start(x_quad[q * Q:(q + 1) * Q, :, :],
                              x_flat[HALF:NT, :].rearrange("(a r) (q c) -> q r a c", r=Q, q=4)[q]
                              ).then_inc(x_half_landed, 16)

        def load_x(eng, c):
            first, after = X_LOADS[c]
            eng.dma_start(x_in[:, first:after, :], x[first:after].rearrange("b t h -> t b h")
                          ).then_inc(x_landed[c], 16)

        def load_first(eng, g):
            eng.dma_start(w_first[0:KL, g, :], gu_w[g][0:F3, :].rearrange("(m j) h -> m j h", j=FT)[:, 0, :]
                          ).then_inc(first_landed[g], 16)
            eng.dma_start(w_first[KL:P, g, :], gu_w[g][F3:F, :].rearrange("(m j) h -> m j h", j=NL)[:, 0, :]
                          ).then_inc(first_landed[g], 16)

        def load_w(eng, landed, g, j, slot, last=False):
            three = gu_w[g][0:F3, :].rearrange("(a r j) (q c) -> q r a j c", a=3, r=Q, q=4)
            four = gu_w[g][F3:F, :].rearrange("(r j) (q c) -> q r j c", r=Q, q=4)
            for q in range(4):
                rows = slice(q * Q, (q + 1) * Q)
                eng.dma_start(w_in[rows, slot, g, 0:3, :], three[q, :, :, j, :]).then_inc(landed, 16)
                if not last:
                    eng.dma_start(w_in[rows, slot, g, 3, :], four[q, :, j, :]).then_inc(landed, 16)

        def load_ids(eng):
            regs = [eng.alloc_register(f"adapter{b}") for b in range(NB)]
            for b in range(0, NB, 4):
                eng.load(regs[b:b + 4], idx_row[0:1, b:b + 4])
            return [eng.snap(reg, min_val=0, max_val=ADAPTERS - 1) for reg in regs]

        def load_b(eng, landed, g, batches, ids):
            for b in batches:
                rows = slice(b // 2 * Q, (b // 2 + 1) * Q)
                src = gu_b[g][0, ids[b]]
                eng.dma_start(b_in[rows, g, b % 2, 0:3 * FT * R].rearrange("p (q c) -> p q c", q=3),
                              src[0:F3, :].rearrange("(q r j) c -> r q (j c)", q=3, r=Q)).then_inc(landed, 16)
                eng.dma_start(b_in[rows, g, b % 2, 3 * FT * R:FB * R],
                              src[F3:F, :].rearrange("(r j) c -> r (j c)", r=Q)).then_inc(landed, 16)

        @block.sync
        def _(sp):
            load_x(sp, 0)
            load_x(sp, 2)
            ids = load_ids(sp)
            load_x_half(sp)
            load_b(sp, b_landed, 0, range(NB), ids)
            load_b(sp, b_landed, 1, range(POOLS_B, NB), ids)
            load_w(sp, w_landed[1], 0, 1, 1)
            load_w(sp, second_landed, 1, 1, 1)
            load_w(sp, w_landed[0], 0, 2, 0)

            def period(tile):
                j, use, slot = tile
                sp.wait_ge(w_tred, j * 2)
                load_w(sp, w_landed[slot], 0, j + 2, slot)

            for j in range(1, PROLOGUE_TILES):
                period(peeled(j))
            with sp.Fori(0, ROUNDS - 1) as i:
                for step in range(2):
                    period(in_loop(i, step))
            period(peeled(FT - 4))
            sp.wait_ge(w_tred, 2 * (FT - 3))
            load_w(sp, w_landed[(FT - 1) % 2], 0, FT - 1, (FT - 1) % 2, last=True)
            sp.wait_ge(b_loed, FT)
            sp.wait_ge(stack_hied, 2 * FT)

            def load_wd(t):
                wd_rows = w_down.rearrange("(q r t) f -> t r q f", q=4, r=Q)[t]
                if t:
                    sp.wait_ge(wd_tred, t)
                for q in range(4):
                    n = FQ if q < 3 else LAST
                    sp.dma_start(wd_in[q * Q:(q + 1) * Q, :, 0:n],
                                 wd_rows[:, :, q * FQ:q * FQ + n]).then_inc(wd_landed, 16)

            load_wd(0)
            load_wd(1)
            load_wd(2)
            sp.wait_ge(td_loed, 2)
            for q in range(4):
                sp.dma_start(wq_int[q * Q:(q + 1) * Q, :, :],
                             wq.rearrange("(b r) (q c) -> q r b c", r=Q, q=4)[q]).then_inc(wq_landed, 16)
            sp.wait_ge(stack_loed, 2 * FT)
            sp.dma_start(bias_t[:, :], bias.rearrange("(a n) -> a n", a=1).broadcast_to([P, H])
                         ).then_inc(bias_landed, 16)

            def load_res(n):
                if n >= 4:
                    sp.wait_ge(out_stored[n % 4], 16 * (n // 4))
                sp.dma_start(res[:, n % 4, :], x_flat[n * P:(n + 1) * P, :]).then_inc(res_landed[n % 4], 16)

            for n in range(4):
                load_res(n)
            load_wd(3)
            for n in range(NB - 1):
                sp.wait_ge(y_added, n + 1)
                sp.dma_start(out_flat[n * P:(n + 1) * P, :], res[:, n % 4, :]).then_inc(out_stored[n % 4], 16)
                if n + 4 < NB:
                    load_res(n + 4)
            for half in range(2):
                cols = slice(half * H // 2, (half + 1) * H // 2)
                sp.wait_ge(y_added, NB + half)
                sp.dma_start(out_flat[NT - P:NT, cols], res[:, 3, cols]).then_inc(out_stored[3], 16)
            for s in range(4):
                sp.wait_ge(out_stored[s], 16 * (NB // 4 + (s == 3)))

        @block.gpsimd
        def _(pool):
            pool.dma_start(idx_all[:, :], idx_row.broadcast_to([P, NB])).then_inc(idx_landed, 16)
            nc.gpsimd.memset(ident[:, :], 0.0).then_inc(consts, 1)
            nc.gpsimd.memset(own[:, :], 1.0).then_inc(consts, 1)
            nc.gpsimd.memset(mask[0:Q, :], LORA_SCALE).then_inc(consts, 1)
            pool.wait_ge(consts, 3)
            nc.gpsimd.affine_select(out=ident[:, :], in_=ident[:, :], compare_op=ALU.not_equal, fill=1.0, base=0,
                                    pattern=[[-1, P]], channel_multiplier=1).then_inc(ident_made, 1)
            nc.gpsimd.affine_select(out=own[:, :], in_=own[:, :], compare_op=ALU.is_ge, fill=0.0, base=0,
                                    pattern=[[-R, NB]], channel_multiplier=1).then_inc(consts, 1)
            pool.wait_ge(consts, 4)
            nc.gpsimd.affine_select(out=own[:, :], in_=own[:, :], compare_op=ALU.is_ge, fill=0.0, base=R - 1,
                                    pattern=[[R, NB]], channel_multiplier=-1).then_inc(consts, 1)
            nc.gpsimd.iota(row_off[:, :], pattern=[[-R, NB]], base=0, channel_multiplier=1,
                           allow_small_or_imprecise_dtypes=True).then_inc(consts, 1)
            nc.gpsimd.affine_select(out=mask[0:Q, 0:T], in_=mask[0:Q, 0:T], compare_op=ALU.is_ge, fill=0.0,
                                    base=R - 1, pattern=[[0, T]], channel_multiplier=-1).then_inc(consts, 1)
            nc.gpsimd.affine_select(out=mask[0:Q, T:PT], in_=mask[0:Q, T:PT], compare_op=ALU.is_ge, fill=0.0,
                                    base=-R, pattern=[[0, T]], channel_multiplier=1).then_inc(consts, 1)
            ids = load_ids(pool)
            pool.wait_ge(rows_made, 4)
            for table, dst, landed in ((a_gate, a_in[:, 0, :], a_landed[0]), (a_up, a_in[:, 1, :], a_landed[1]),
                                       (a_down, ad_rows[:, :], ad_landed)):
                pool.indirect_dma_start(
                    out=dst, out_offset=None, in_=table.rearrange("l a r n -> (l a r) n"),
                    in_offset=bass.IndirectOffsetOnAxis(ap=row_id[:, 0:1], axis=0)).then_inc(landed, 16)
            load_b(pool, b_up_landed, 1, range(POOLS_B), ids)
            load_w(pool, up_landed[0], 1, 2, 0)

            def period(tile):
                j, use, slot = tile
                pool.wait_ge(w_tred, j * 2)
                load_w(pool, up_landed[slot], 1, j + 2, slot)

            for j in range(1, PROLOGUE_TILES):
                period(peeled(j))
            for b in range(NB):
                pool.dma_start(bd_in[KL:P, b // 2, b % 2, :, :],
                               b_down[0, ids[b]].rearrange("(q r t) c -> r q (t c)", q=4, r=Q)).then_inc(bd_landed, 16)
            with pool.Fori(0, ROUNDS - 1) as i:
                for step in range(2):
                    period(in_loop(i, step))
            period(peeled(FT - 4))
            pool.wait_ge(w_tred, 2 * (FT - 3))
            load_w(pool, up_landed[(FT - 1) % 2], 1, FT - 1, (FT - 1) % 2, last=True)
            for q in range(4):
                for src, dst in ((scale, scale_t), (zero_point, zero_t)):
                    pool.dma_start(dst[q * Q:(q + 1) * Q, :], src.rearrange("(b r) g -> g r b", r=Q)[q],
                                   allow_slow_non_contiguous=True).then_inc(sz_landed, 16)
            pool.wait_ge(bias_landed, 16)
            for n in range(NB):
                pool.wait_ge(res_landed[n % 4], 16 * (n // 4 + 1))
                nc.gpsimd.tensor_tensor(res[:, n % 4, :], res[:, n % 4, :], bias_t[:, :], ALU.add).then_inc(biased, 1)

        @block.scalar
        def _(act):
            def x_part(banks):
                for c in banks:
                    act.wait_ge(x_tred, c + 1)
                    nc.scalar.copy(x_bank(xt_hi, c), x_ps[c][:, :].rearrange("p (k t) -> p k t", k=2)
                                   ).then_inc(x_hied, 1)

            def x_half_part(tiles):
                for k in tiles:
                    act.wait_ge(x_half_tred, k + 1)
                    nc.scalar.copy(xt_hi[:, k, HALF:NT], x_tr[:, k, :]).then_inc(x_hied, 1)

            def w_part(tile, quads=4):
                j, use, slot = tile
                for g in range(2):
                    act.wait_ge(w_tred, j * 2 + (g - 1))
                    nc.scalar.copy(w_hi[:, slot, g, :, 0:quads * Q], w_tr[:, g, :, 0:quads * Q]).then_inc(w_hied, 1)

            def b_part(tile, quads=4):
                j, use, slot = tile
                m = quads * Q
                src = b_tr[:, :, 0:quads * FQ].rearrange("p g (q j r) -> p g q j r", q=quads, j=FT)[:, :, :, j, :]

                def by_quad(ap):
                    return ap.rearrange("p g (q r) -> p g q r", q=quads)

                nc.scalar.copy(by_quad(b_hi[:, :, 0:m]), src).then_inc(b_hied, 1)
                for p in range(PAIRS):
                    for s in range(2):
                        last = nc.scalar.copy(by_quad(b_stack[s * Q:(s + 1) * Q, slot, p, :, 0:m]),
                                              src[p * Q:(p + 1) * Q])
                    if p % 2 == 1:
                        last.then_inc(stack_hied, 1)

            def t_part(h):
                act.wait_ge(bank_read, h + 1)
                nc.scalar.copy(t_hi[:, h, :], t_val[:, h, :]).then_inc(t_hied, 1)
                for p in range(2):
                    for g in range(2):
                        last = nc.scalar.copy(t_stack[0:Q, g, h * HALF + p * PT:h * HALF + (p + 1) * PT],
                                              t_val[(2 * p + g) * Q:(2 * p + g + 1) * Q, h, :])
                last.then_inc(ts_hied, 1)

            def ad_part(j, slot):
                nc.scalar.copy(ad_parts[:, slot, :, :, 0, :],
                               ad_tr[:, :, j, :].rearrange("p (h a) r -> p h a r", h=2)).then_inc(ad_hied, 1)

            def ad_last():
                act.wait_ge(unit_done, 2 * (FT - 1))
                nc.scalar.copy(ad_tail[0:KL, :, :, 0, :],
                               ad_tr[0:KL, :, FT - 1, :].rearrange("p (h a) r -> p h a r", h=2)).then_inc(ad_hied, 1)

            def silu_part(j, h, rows=P):
                act.wait_ge(gate_done, j * 2 + (h + 1))
                nc.scalar.activation(silu[0:rows, h, :], gate_ps[h][0:rows, :], ACT.Silu).then_inc(silu_done, 1)

            def act_part(j, h, rows=P):
                act.wait_ge(act_done, j * 2 + (h + 1))
                nc.scalar.copy(act_hi[0:rows, j, h * HALF:(h + 1) * HALF], actf[0:rows, h, :]).then_inc(act_hied, 1)

            act.wait_ge(scratch_set, 1)
            nc.scalar.activation(silu[0:1, 0, P:P + 1], silu[0:1, 0, 0:1], ACT.Silu)
            load_x(act, 1)
            load_first(act, 0)
            load_first(act, 1)
            x_part(range(3))
            for g in range(2):
                if g == 1:
                    x_part(range(3, 4))
                act.wait_ge(first_tred, g + 1)
                nc.scalar.copy(w_hi[:, 0, g, :, :], w_ps[g][:, :].rearrange("p (k m) -> p k m", k=KT)
                               ).then_inc(w_hied, 1)
            x_half_part(range(2))
            for g in range(2):
                act.wait_ge(a_tred, g + 1)
                nc.scalar.copy(a_hi[:, :, :, g, :],
                               a_ps[g][:, :].rearrange("p (k a c) -> p k a c", k=KT, a=PAIRS)).then_inc(a_hied, 1)
            x_half_part(range(2, 4))
            act.wait_ge(ad_landed, 16)
            for q in range(1, 4):
                n = FQ if q < 3 else LAST
                for p in range(PAIRS):
                    last = nc.scalar.copy(ad_in[q * Q:(q + 1) * Q, p, 0:n],
                                          ad_rows[p * Q:(p + 1) * Q, q * FQ:q * FQ + n])
            last.then_inc(ad_copied, 1)
            t_part(0)
            act.wait_ge(b_tred, 2)
            b_part(peeled(0))
            t_part(1)

            def first_period(j):
                after = peeled(j + 1)
                if j == 0:
                    silu_part(j, 0)
                    w_part(after)
                    act_part(j, 0)
                    silu_part(j, 1)
                else:
                    act.wait_ge(unit_done, 2 * j)
                    w_part(after)
                    silu_part(j, 0)
                    act_part(j, 0)
                act.wait_ge(b_tred, 2 * j + 4)
                b_part(after)
                if j:
                    act.wait_ge(ad_tred, 2)
                    ad_part(j - 1, j - 1)
                    silu_part(j, 1)
                act_part(j, 1)

            def period(tile, after, quads=4):
                j, use, slot = tile
                act.wait_ge(unit_done, j * 2)
                w_part(after, quads)
                b_part(after, quads)
                act.wait_ge(td_used, j - 2)
                ad_part(j - 1, 1 - slot)
                for h in range(2):
                    silu_part(j, h)
                    act_part(j, h)

            for j in range(PROLOGUE_TILES):
                first_period(j)
            with act.Fori(0, ROUNDS) as i:
                for step in range(2):
                    period(in_loop(i, step), in_loop(i, step + 1))
            period(peeled(FT - 2), peeled(FT - 1), 3)

            def wd_part(t):
                act.wait_ge(wd_tred, t + 1)
                s = t % 2
                nc.scalar.copy(wl_hi[s][KL:P, :, :], bd_tr[KL:P, :, t, :])
                nc.scalar.copy(wl_hi[s][0:KL, :, :],
                               wd_tr[0:KL, FT - 1:FT, :].broadcast_to([KL, PAIRS, P]))
                nc.scalar.copy(wd_hi[s][:, :, :], wd_tr[:, 0:FT - 1, :]).then_inc(wd_hied, 1)

            act.wait_ge(td_used, FT - 3)
            ad_part(FT - 2, (FT - 2) % 2)
            ad_last()
            silu_part(FT - 1, 0, KL)
            wd_part(0)
            act_part(FT - 1, 0, KL)
            silu_part(FT - 1, 1, KL)
            act_part(FT - 1, 1, KL)

            def td_copy(h):
                act.wait_ge(td_done, h + 1)
                for p in range(2):
                    cols = slice(p * PT, (p + 1) * PT)
                    nc.scalar.copy(td_a[h][KL:P, cols], td_ps[h][2 * p * Q:(2 * p + 1) * Q, cols])
                    last = nc.scalar.copy(td_b[h][KL:P, cols], td_ps[h][(2 * p + 1) * Q:(2 * p + 2) * Q, cols])
                last.then_inc(td_copied, 1)

            def td_part(h):
                act.wait_ge(td_masked, h + 1)
                nc.scalar.copy(act_hi[KL:P, FT - 1, h * HALF:(h + 1) * HALF], td_a[h][KL:P, :]).then_inc(td_hied, 1)

            def down_part(t, h):
                act.wait_ge(down_done, 2 * t + h + 1)
                nc.scalar.copy(dt_hi[:, t, h * HALF:(h + 1) * HALF], down_ps[h][:, :]).then_inc(down_hied, 1)

            td_copy(0)
            td_part(0)
            td_copy(1)
            wd_part(1)
            td_part(1)
            for h in range(2):
                down_part(0, h)
            for t in range(1, KT - 1):
                wd_part(t + 1)
                down_part(t, 0)
                if t == KT - 2:
                    for tq in range(KT):
                        act.wait_ge(wq_tred, tq + 1)
                        nc.scalar.copy(wq_hi[:, tq, :], wq_tr[:, tq % 2, :]).then_inc(wq_hied, 1)
                down_part(t, 1)
            for h in range(2):
                down_part(KT - 1, h)

        @block.vector
        def _(dve):
            SUB = ALU.subtract

            def x_part(banks):
                for c in banks:
                    dve.wait_ge(x_hied, c + 1)
                    nc.vector.tensor_tensor(x_bank(xt_lo, c), x_ps[c][:, :].rearrange("p (k t) -> p k t", k=2),
                                            x_bank(xt_hi, c).bitcast(F32), SUB).then_inc(x_loed, 1)

            def x_half_transpose():
                dve.wait_ge(x_half_landed, 4 * 16)
                for k in range(KT):
                    nc.vector.transpose(x_tr[:, k, :].rearrange("p (a r) -> p a r", r=Q),
                                        x_quad[:, :, :].rearrange("p a (r k) -> p a k r", k=KT)[:, :, k]
                                        ).then_inc(x_half_tred, 1)

            def x_half_part():
                for k in range(KT):
                    dve.wait_ge(x_hied, 4 + k + 1)
                    nc.vector.tensor_tensor(xt_lo[:, k, HALF:NT], x_tr[:, k, :], xt_hi[:, k, HALF:NT].bitcast(F32),
                                            SUB).then_inc(x_loed, 1)

            def w_transpose(tile, quads=4, gates=(0, 1)):
                j, use, slot = tile
                last = W_LOAD if quads == 4 else W_LAST
                for g in gates:
                    if g == 0:
                        dve.wait_ge(w_landed[slot], (use - 1) * W_LOAD + last)
                    elif isinstance(j, int) and j == 1:
                        dve.wait_ge(second_landed, W_LOAD)
                    else:
                        dve.wait_ge(up_landed[slot], (use - slot - 1) * W_LOAD + last)
                    nc.vector.transpose(
                        w_tr[:, g, :, 0:quads * Q].rearrange("p k (a r) -> p a k r", r=Q),
                        w_in[:, slot, g, 0:quads, :].rearrange("p a (r k) -> p a k r", k=KT)).then_inc(w_tred, 1)

            def w_part(tile, quads=4, gates=(0, 1)):
                j, use, slot = tile
                for g in gates:
                    dve.wait_ge(w_hied, j * 2 + (g + 1))
                    m = quads * Q
                    nc.vector.tensor_tensor(w_lo[:, slot, g, :, 0:m], w_tr[:, g, :, 0:m],
                                            w_hi[:, slot, g, :, 0:m].bitcast(F32), SUB).then_inc(w_loed, 1)

            def b_part(tile, quads=4):
                j, use, slot = tile
                dve.wait_ge(b_hied, j + 1)
                m = quads * Q
                src = b_tr[:, :, 0:quads * FQ].rearrange("p g (q j r) -> p g q j r", q=quads, j=FT)[:, :, :, j, :]

                def by_quad(ap):
                    return ap.rearrange("p g (q r) -> p g q r", q=quads)

                nc.vector.tensor_tensor(by_quad(b_lo[:, :, 0:m]), src, by_quad(b_hi[:, :, 0:m]).bitcast(F32),
                                        SUB).then_inc(b_loed, 1)
                dve.wait_ge(b_loed, j + 1)
                for p in range(PAIRS):
                    last = nc.vector.tensor_copy(b_stack[2 * Q:3 * Q, slot, p, :, 0:m],
                                                 b_lo[p * Q:(p + 1) * Q, :, 0:m].bitcast(F32))
                    if p % 2 == 1:
                        last.then_inc(stack_loed, 1)

            def ad_part(j, slot):
                dve.wait_ge(ad_hied, j + 1)
                nc.vector.tensor_tensor(ad_parts[:, slot, :, :, 1, :],
                                        ad_tr[:, :, j, :].rearrange("p (h a) r -> p h a r", h=2),
                                        ad_parts[:, slot, :, :, 0, :].bitcast(F32), SUB).then_inc(ad_loed, 1)

            def up_part(j, h, rows=P):
                dve.wait_ge(silu_done, j * 2 + (h + 1))
                dve.wait_ge(unit_done, j * 2 + (h + 1))
                nc.vector.tensor_tensor(actf[0:rows, h, :], up_ps[h][0:rows, :], silu[0:rows, h, :],
                                        ALU.mult).then_inc(act_done, 1)

            def act_part(j, h, rows=P):
                dve.wait_ge(act_hied, j * 2 + (h + 1))
                cols = slice(h * HALF, (h + 1) * HALF)
                nc.vector.tensor_tensor(act_lo[0:rows, j, cols], actf[0:rows, h, :],
                                        act_hi[0:rows, j, cols].bitcast(F32), SUB).then_inc(act_loed, 1)

            def t_mask(h):
                dve.wait_ge(t_done, h + 1)
                for p in range(2):
                    rows = slice(2 * p * Q, 2 * (p + 1) * Q)
                    last = nc.vector.tensor_tensor(t_val[rows, h, :], t_ps[h][rows, p * PT:(p + 1) * PT],
                                                   mask[rows, :], ALU.mult)
                last.then_inc(bank_read, 1)

            def t_part(h):
                dve.wait_ge(bank_read, h + 1)
                for p in range(2):
                    for g in range(2):
                        nc.vector.tensor_copy(t_stack[2 * Q:KL, g, h * HALF + p * PT:h * HALF + (p + 1) * PT],
                                              t_val[(2 * p + g) * Q:(2 * p + g + 1) * Q, h, :])
                dve.wait_ge(t_hied, h + 1)
                nc.vector.tensor_tensor(t_lo[:, h, :], t_val[:, h, :], t_hi[:, h, :].bitcast(F32),
                                        SUB).then_inc(t_loed, 1)
                dve.wait_ge(t_loed, h + 1)
                for p in range(2):
                    for g in range(2):
                        last = nc.vector.tensor_copy(
                            t_stack[Q:2 * Q, g, h * HALF + p * PT:h * HALF + (p + 1) * PT],
                            t_lo[(2 * p + g) * Q:(2 * p + g + 1) * Q, h, :].bitcast(F32))
                last.then_inc(ts_loed, 1)

            def b_transpose(first, step=1):
                for g in range(2):
                    nc.vector.transpose(b_tr[:, g, 0:F].rearrange("p (b r) -> p b r", r=Q)[:, first:FB:step],
                                        b_in[:, g, :, :].rearrange("p e (b c) -> p b e c", c=R)[:, first:FB:step]
                                        ).then_inc(b_tred, 1)

            def ad_move(q):
                n = FQ if q < 3 else LAST
                for p in range(PAIRS):
                    nc.vector.tensor_copy(ad_in[q * Q:(q + 1) * Q, p, 0:n],
                                          ad_rows[p * Q:(p + 1) * Q, q * FQ:q * FQ + n]).then_inc(ad_moved, 1)

            nc.vector.memset(silu[:, 0, 0:P], 0.0).then_inc(scratch_set, 1)
            dve.wait_ge(consts, 8)
            dve.wait_ge(idx_landed, 16)
            nc.vector.scalar_tensor_tensor(out=row_all[:, :], in0=idx_all[:, :], scalar=float(R), in1=row_off[:, :],
                                           op0=ALU.mult, op1=ALU.add).then_inc(rows_made, 1)
            dve.wait_ge(rows_made, 1)
            nc.vector.tensor_tensor(row_own[:, :], row_all[:, :], own[:, :], ALU.mult).then_inc(rows_made, 1)
            dve.wait_ge(rows_made, 2)
            nc.vector.reduce_sum(row_sum[:, 0:1], row_own[:, :], axis=mybir.AxisListType.X).then_inc(rows_made, 1)
            dve.wait_ge(rows_made, 3)
            nc.vector.tensor_copy(row_id[:, 0:1], row_sum[:, 0:1]).then_inc(rows_made, 1)
            x_part(range(3))
            for g in range(2):
                if g == 1:
                    x_part(range(3, 4))
                dve.wait_ge(w_hied, g + 1)
                nc.vector.tensor_tensor(w_lo[:, 0, g, :, :], w_ps[g][:, :].rearrange("p (k m) -> p k m", k=KT),
                                        w_hi[:, 0, g, :, :].bitcast(F32), SUB).then_inc(w_loed, 1)
            x_half_transpose()
            for g in range(2):
                dve.wait_ge(a_hied, g + 1)
                nc.vector.tensor_tensor(a_lo[:, :, :, g, :],
                                        a_ps[g][:, :].rearrange("p (k a c) -> p k a c", k=KT, a=PAIRS),
                                        a_hi[:, :, :, g, :].bitcast(F32), SUB).then_inc(a_loed, 1)
            x_half_part()
            for q in range(1, 4):
                last = nc.vector.tensor_copy(mask[q * Q:(q + 1) * Q, :], mask[0:Q, :])
            last.then_inc(mask_made, 1)
            dve.wait_ge(ad_landed, 16)
            ad_move(0)
            dve.wait_ge(mask_made, 1)
            t_mask(0)
            t_part(0)
            dve.wait_ge(b_landed, (2 * NB - POOLS_B) * B_LOAD)
            dve.wait_ge(b_up_landed, POOLS_B * B_LOAD)
            b_transpose(0, FT)
            t_mask(1)
            b_part(peeled(0))
            t_part(1)

            def ad_transpose(rows, blocks):
                for a in range(PAIRS):
                    last = nc.vector.transpose(ad_tr[rows, a, 0:blocks, :],
                                               ad_in[rows, a, 0:blocks * Q].rearrange("p (r j) -> p j r", j=blocks))
                last.then_inc(ad_tred, 1)

            def first_period(j):
                after = peeled(j + 1)
                if j == 0:
                    for g in range(2):
                        w_transpose(after, gates=(g,))
                        if g == 0:
                            up_part(j, 0)
                        w_part(after, gates=(g,))
                else:
                    w_transpose(after)
                    act_part(j - 1, 1)
                    w_part(after)
                    up_part(j, 0)
                if j < PROLOGUE_TILES - 1:
                    b_transpose(j + 1, FT)
                else:
                    dve.wait_ge(stack_hied, 2 * (j + 1))
                    dve.wait_ge(b_loed, j + 1)
                    b_transpose(j + 1)
                act_part(j, 0)
                b_part(after)
                if j == 0:
                    up_part(j, 1)
                    dve.wait_ge(ad_moved, PAIRS)
                    dve.wait_ge(ad_copied, 1)
                    ad_transpose(slice(0, KL), FT)
                else:
                    if j == 1:
                        ad_transpose(slice(KL, P), NL)
                    ad_part(j - 1, j - 1)
                    up_part(j, 1)

            def period(tile, after):
                j, use, slot = tile
                w_transpose(after)
                w_part(after)
                b_part(after)
                ad_part(j - 1, 1 - slot)
                for h in range(2):
                    up_part(j, h)
                    act_part(j, h)

            def last_period():
                j, after = FT - 2, peeled(FT - 1)
                w_transpose(after, 3)
                w_part(after, 3)
                b_part(after, 3)
                ad_part(j - 1, (j - 1) % 2)
                up_part(j, 0)
                act_part(j, 0)
                dve.wait_ge(bd_landed, NB * 16)
                for a in range(PAIRS):
                    for t in range(KT):
                        nc.vector.transpose(
                            bd_tr[KL:P, a, t, :].rearrange("p (q r) -> p q r", q=4),
                            bd_in[KL:P, a, :, :, t * R:(t + 1) * R].rearrange("p e q c -> p q e c"))
                up_part(j, 1)
                act_part(j, 1)

            for j in range(PROLOGUE_TILES):
                first_period(j)
            act_part(PROLOGUE_TILES - 1, 1)
            with dve.Fori(0, ROUNDS) as i:
                for step in range(2):
                    period(in_loop(i, step), in_loop(i, step + 1))
            last_period()

            def wd_transpose(t):
                dve.wait_ge(wd_landed, (t + 1) * 4 * 16)
                if t:
                    dve.wait_ge(wd_loed, t)
                if t == 1:
                    dve.wait_ge(unit_done, 2 * FT)
                if t >= 2:
                    dve.wait_ge(down_done, 2 * (t - 1))
                for q in range(4):
                    cols = slice(q * Q, (q + 1) * Q)
                    nc.vector.transpose(wd_tr[0:KL, :, cols], wd_in[0:KL, q, :].rearrange("p (r j) -> p j r", j=FT))
                    last = nc.vector.transpose(wd_tr[KL:P, 0:NL, cols],
                                               wd_in[KL:P, q, 0:LAST].rearrange("p (r j) -> p j r", j=NL))
                last.then_inc(wd_tred, 1)

            def wd_part(t):
                s = t % 2
                dve.wait_ge(wd_hied, t + 1)
                nc.vector.tensor_tensor(wl_lo[s][KL:P, :, :], bd_tr[KL:P, :, t, :],
                                        wl_hi[s][KL:P, :, :].bitcast(F32), SUB)
                nc.vector.tensor_tensor(wl_lo[s][0:KL, :, :], wd_tr[0:KL, FT - 1:FT, :].broadcast_to([KL, PAIRS, P]),
                                        wl_hi[s][0:KL, :, :].bitcast(F32), SUB)
                nc.vector.tensor_tensor(wd_lo[s][:, :, :], wd_tr[:, 0:FT - 1, :], wd_hi[s][:, :, :].bitcast(F32),
                                        SUB).then_inc(wd_loed, 1)

            ad_part(FT - 2, (FT - 2) % 2)
            dve.wait_ge(ad_hied, FT)
            nc.vector.tensor_tensor(ad_tail[0:KL, :, :, 1, :],
                                    ad_tr[0:KL, :, FT - 1, :].rearrange("p (h a) r -> p h a r", h=2),
                                    ad_tail[0:KL, :, :, 0, :].bitcast(F32), SUB).then_inc(ad_loed, 1)
            wd_transpose(0)
            up_part(FT - 1, 0, KL)
            wd_part(0)
            act_part(FT - 1, 0, KL)
            up_part(FT - 1, 1, KL)
            act_part(FT - 1, 1, KL)

            def td_mask(h):
                dve.wait_ge(td_copied, h + 1)
                nc.vector.tensor_tensor(td_a[h][KL:P, :], td_a[h][KL:P, :], td_b[h][KL:P, :],
                                        ALU.add).then_inc(td_summed, 1)
                dve.wait_ge(td_summed, h + 1)
                for p in range(2):
                    cols = slice(p * PT, (p + 1) * PT)
                    last = nc.vector.tensor_tensor(td_a[h][KL:P, cols], td_a[h][KL:P, cols], mask[KL:P, :], ALU.mult)
                last.then_inc(td_masked, 1)

            def td_part(h):
                dve.wait_ge(td_hied, h + 1)
                cols = slice(h * HALF, (h + 1) * HALF)
                nc.vector.tensor_tensor(act_lo[KL:P, FT - 1, cols], td_a[h][KL:P, :],
                                        act_hi[KL:P, FT - 1, cols].bitcast(F32), SUB).then_inc(td_loed, 1)

            def down_part(t, h):
                dve.wait_ge(down_hied, 2 * t + h + 1)
                cols = slice(h * HALF, (h + 1) * HALF)
                nc.vector.tensor_tensor(dt_lo[:, t, cols], down_ps[h][:, :], dt_hi[:, t, cols].bitcast(F32),
                                        SUB).then_inc(bank_read, 1)

            def wq_value():
                dve.wait_ge(wq_landed, 4 * 16)
                dve.wait_ge(sz_landed, 2 * 4 * 16)
                nc.vector.tensor_tensor(wq_val[:, :, :], wq_int[:, :, :],
                                        zero_t[:, :].unsqueeze(2).broadcast_to([P, 16, P]), SUB).then_inc(wq_zeroed, 1)
                dve.wait_ge(wq_zeroed, 1)
                nc.vector.tensor_tensor(wq_val[:, :, :], wq_val[:, :, :],
                                        scale_t[:, :].unsqueeze(2).broadcast_to([P, 16, P]), ALU.mult
                                        ).then_inc(wq_scaled, 1)

            def wq_part():
                dve.wait_ge(wq_scaled, 1)
                for t in range(KT):
                    nc.vector.transpose(wq_tr[:, t % 2, :].rearrange("p (b r) -> p b r", r=Q),
                                        wq_val[:, :, :].rearrange("p b (r t) -> p b r t", t=KT)[:, :, :, t]
                                        ).then_inc(wq_tred, 1)
                    dve.wait_ge(wq_hied, t + 1)
                    nc.vector.tensor_tensor(wq_lo[:, t, :], wq_tr[:, t % 2, :], wq_hi[:, t, :].bitcast(F32),
                                            SUB).then_inc(wq_loed, 1)

            td_mask(0)
            td_part(0)
            wd_transpose(1)
            td_mask(1)
            wd_part(1)
            td_part(1)
            for h in range(2):
                down_part(0, h)
            for t in range(1, KT - 1):
                wd_transpose(t + 1)
                wd_part(t + 1)
                down_part(t, 0)
                if t == 1:
                    wq_value()
                if t == KT - 2:
                    wq_part()
                down_part(t, 1)
            for h in range(2):
                down_part(KT - 1, h)
            for n in range(NB - 1):
                dve.wait_ge(y_done, n + 1)
                dve.wait_ge(biased, n + 1)
                nc.vector.tensor_tensor(res[:, n % 4, :], y_ps[n % 4][:, :], res[:, n % 4, :],
                                        ALU.add).then_inc(y_added, 1)
            dve.wait_ge(biased, NB)
            for half in range(2):
                cols = slice(half * H // 2, (half + 1) * H // 2)
                dve.wait_ge(y_done, NB + half)
                nc.vector.tensor_tensor(res[:, 3, cols], y_ps[3 * (1 - half)][:, cols], res[:, 3, cols],
                                        ALU.add).then_inc(y_added, 1)

        @block.tensor
        def _(pe):
            mm = nc.tensor.matmul

            def project_t(h):
                pe.wait_ge(x_loed, KT * (h + 1))
                pe.wait_ge(a_loed, 2)
                cols = slice(h * HALF, (h + 1) * HALF)
                n = 0
                for w, v in ((a_hi, xt_hi), (a_hi, xt_lo), (a_lo, xt_hi)):
                    for k in range(KT):
                        last = mm(t_ps[h][:, :], w[:, k, 2 * h:2 * h + 2, :, :], v[:, k, cols],
                                  start=n == 0, stop=n == 3 * KT - 1)
                        n += 1
                last.then_inc(t_done, 1)

            products = [(w, v, k) for w, v in ((w_hi, xt_hi), (w_lo, xt_hi), (w_hi, xt_lo)) for k in range(KT)]

            def weights(tile, h, m=P, gates=(0, 1)):
                j, use, slot = tile
                first = isinstance(j, int) and j == 0
                if first:
                    pe.wait_ge(x_hied, 4 * h + 3)
                    if h == 1 or gates[0] == 1:
                        pe.wait_ge(x_loed, 4)
                else:
                    pe.wait_ge(act_done, j * 2 + (h - 1))
                for g in gates:
                    ps = (gate_ps[h], up_ps[h])[g]
                    pe.wait_ge(w_hied, j * 2 + (g + 1))
                    for n, (w, v, k) in enumerate(products[:-1]):
                        if first and n == 2:
                            pe.wait_ge(x_hied, 4 * (h + 1))
                        if n == KT:
                            pe.wait_ge(w_loed, j * 2 + (g + 1))
                        if first and n == 2 * KT:
                            pe.wait_ge(x_loed, 4 * (h + 1))
                        mm(ps[0:m, :], w[:, slot, g, k, 0:m], v[:, k, h * HALF:(h + 1) * HALF],
                           start=n == 0, stop=False)

            def adapters(tile, h, m=P):
                j, use, slot = tile
                pe.wait_ge(stack_hied, j * 2 + (h + 1))
                pe.wait_ge(stack_loed, j * 2 + (h + 1))
                pe.wait_ge(ts_hied, h + 1)
                pe.wait_ge(ts_loed, h + 1)
                w, v, k = products[-1]
                for g, ps in enumerate((gate_ps[h], up_ps[h])):
                    for p in range(2):
                        toks = slice(h * HALF + p * PT, h * HALF + (p + 1) * PT)
                        mm(ps[0:m, p * PT:(p + 1) * PT], b_stack[0:KL, slot, 2 * h + p, g, 0:m],
                           t_stack[0:KL, g, toks], start=False, stop=False, skip_group_check=True)
                    last = mm(ps[0:m, :], w[:, slot, g, k, 0:m], v[:, k, h * HALF:(h + 1) * HALF],
                              start=False, stop=True)
                    if g == 0:
                        last.then_inc(gate_done, 1)
                last.then_inc(unit_done, 1)

            def project_act(j, w, h, rows=P, first=False, last_tile=False):
                pe.wait_ge(act_hied if last_tile else act_loed, j * 2 + (h + 1))
                pe.wait_ge(ad_loed, j + 1)
                cols = slice(h * HALF, (h + 1) * HALF)
                w = w[0:rows, h, :, :, :]
                mm(td_ps[h][:, :], w, act_hi[0:rows, j, cols], start=first, stop=False, skip_group_check=True)
                if last_tile:
                    pe.wait_ge(act_loed, j * 2 + (h + 1))
                last = mm(td_ps[h][:, :], w, act_lo[0:rows, j, cols], start=False, stop=last_tile,
                          skip_group_check=True)
                if last_tile:
                    last.then_inc(td_done, 1)
                elif h == 1:
                    last.then_inc(td_used, 1)

            def transpose(ps, c, rows):
                return nc.tensor.transpose(ps[:, c * P:(c + 1) * P], rows, ident[:, :])

            def tile_of(ap, k):
                return ap.rearrange("p (m k) -> p k m", k=KT)[:, k]

            def transpose_x(banks):
                for c in banks:
                    for b in range(2):
                        batch = c // 2 * 2 + b
                        for n, (first, after) in enumerate(X_LOADS):
                            if first == batch and c % 2 == 0:
                                pe.wait_ge(x_landed[n], 16)
                        for k in range(2):
                            last = transpose(x_ps[c], 2 * k + b, tile_of(x_in[:, batch, :], 2 * (c % 2) + k))
                    last.then_inc(x_tred, 1)

            def transpose_first(g):
                pe.wait_ge(first_landed[g], 2 * 16)
                for k in range(KT):
                    last = transpose(w_ps[g], k, tile_of(w_first[:, g, :], k))
                last.then_inc(first_tred, 1)

            pe.wait_ge(scratch_set, 1)
            for _ in range(WARM_UPS):
                mm(gate_ps[0][:, 0:P], silu[:, 0, 0:P], silu[:, 0, 0:P], start=True, stop=True)
            pe.wait_ge(ident_made, 1)
            transpose_x(range(3))
            transpose_first(0)
            transpose_x(range(3, 4))
            transpose_first(1)
            weights(peeled(0), 0, gates=(0,))
            for g in range(2):
                if g == 1:
                    pe.wait_ge(w_loed, 2)
                pe.wait_ge(a_landed[g], 16)
                for k in range(KT):
                    last = transpose(a_ps[g], k, tile_of(a_in[:, g, :], k))
                last.then_inc(a_tred, 1)
            weights(peeled(0), 0, gates=(1,))
            project_t(0)
            project_t(1)
            weights(peeled(0), 1, gates=(0,))
            adapters(peeled(0), 0)
            weights(peeled(0), 1, gates=(1,))
            adapters(peeled(0), 1)

            for h in range(2):
                weights(peeled(1), h)
                adapters(peeled(1), h)
            for h in range(2):
                weights(peeled(2), h)
                adapters(peeled(2), h)
            for h in range(2):
                project_act(0, ad_parts[:, 0], h, first=True)
            with pe.Fori(0, ROUNDS) as i:
                for step in range(2):
                    tile = in_loop(i, step)
                    for h in range(2):
                        weights(tile, h)
                        adapters(tile, h)
                        project_act(i * 2 + (PROLOGUE_TILES + step - 2), ad_parts[:, tile[2]], h)
            for h in range(2):
                weights(peeled(FT - 2), h)
                adapters(peeled(FT - 2), h)
                project_act(FT - 4, ad_parts[:, FT % 2], h)
            for h in range(2):
                weights(peeled(FT - 1), h, KL)
                adapters(peeled(FT - 1), h, KL)
            for j in (FT - 3, FT - 2):
                for h in range(2):
                    project_act(j, ad_parts[:, j % 2], h)
            for h in range(2):
                project_act(FT - 1, ad_tail, h, rows=KL, last_tile=True)

            with pe.Fori(0, KT // 2) as i:
                for s in range(2):
                    for h in range(2):
                        group = i * 4 + (2 * s + h)
                        cols = slice(h * HALF, (h + 1) * HALF)
                        pe.wait_ge(wd_loed, i * 2 + (s + 1))
                        pe.wait_ge(bank_read, group + 1)
                        products = [(w, v, j) for w, v in ((wd_hi, act_hi), (wd_hi, act_lo), (wd_lo, act_hi))
                                    for j in range(FT - 1)]
                        for n, (w, v, j) in enumerate(products[:-1]):
                            mm(down_ps[h][:, :], w[s][:, j, :], v[:, j, cols], start=n == 0, stop=False)
                        pe.wait_ge(td_loed, h + 1)
                        for p in range(2):
                            toks = slice(h * HALF + p * PT, h * HALF + (p + 1) * PT)
                            for w, v in ((wl_hi, act_hi), (wl_hi, act_lo), (wl_lo, act_hi)):
                                mm(down_ps[h][:, p * PT:(p + 1) * PT], w[s][:, 2 * h + p, :],
                                   v[:, FT - 1, toks], start=False, stop=False, skip_group_check=True)
                        w, v, j = products[-1]
                        last = mm(down_ps[h][:, :], w[s][:, j, :], v[:, j, cols], start=False, stop=True)
                        last.then_inc(down_done, 1)

            pe.wait_ge(wq_loed, KT)

            def token_tile(n, ps, cols):
                toks = slice(n * P, (n + 1) * P)
                c = 0
                for v, w in ((dt_hi, wq_hi), (dt_hi, wq_lo), (dt_lo, wq_hi)):
                    for t in range(KT):
                        last = mm(ps[:, cols], v[:, t, toks], w[:, t, cols], start=c == 0, stop=c == 3 * KT - 1)
                        c += 1
                last.then_inc(y_done, 1)

            for n in range(NB - 1):
                pe.wait_ge(bank_read, 2 + 2 * KT - 1 + n // (NB // 2))
                if n >= 4:
                    pe.wait_ge(y_added, n - 3)
                token_tile(n, y_ps[n % 4], slice(0, H))
            for half in range(2):
                pe.wait_ge(y_added, 4 + half)
                token_tile(NB - 1, y_ps[3 * (1 - half)], slice(half * H // 2, (half + 1) * H // 2))


_INS = ['x', 'itok_B_2_6', 'L0_cond_W_gate', 'L0_cond_W_up', 'L0_cond_W_down', 'L0_cond_A_gate', 'L0_cond_B_gate',
        'L0_cond_A_up', 'L0_cond_B_up', 'L0_cond_A_down', 'L0_cond_B_down', 'L0_ffn_weight_q', 'L0_ffn_scale',
        'L0_ffn_zero_point', 'L0_ffn_bias']
_OUT = ((NB, T, H), 'float32')


def kernel(**inputs):
    import numpy as _np
    import concourse.bacc as _bacc
    from concourse import mybir as _mybir
    from concourse.bass_utils import run_bass_kernel_spmd as _run

    nc = _bacc.Bacc("TRN2", target_bir_lowering=False, num_devices=1)
    arrays, args = {}, []
    for name in _INS:
        a = _np.ascontiguousarray(inputs[name])
        arrays[f"in_{name}"] = a
        args.append(nc.dram_tensor(f"in_{name}", a.shape, _mybir.dt.from_np(a.dtype), kind="ExternalInput").ap())
    out = nc.dram_tensor("out_y", _OUT[0], _mybir.dt.from_np(_np.dtype(_OUT[1])), kind="ExternalOutput").ap()
    adaln_ffn(nc, *args, out)
    r = _run(nc, [arrays], core_ids=[0])
    return r.results[0]["out_y"]
```
